# Optimizing a Trainium2 kernel written in Bass

```python
import numpy as np
import jax
import jax.numpy as jnp

def _softmax(x, axis=-1):
    return jax.nn.softmax(x, axis=axis)

def _gelu(x):
    return jax.nn.gelu(x, approximate=True)

def _silu(x):
    return jax.nn.silu(x)

def _sigmoid(x):
    return jax.nn.sigmoid(x)

def _layernorm(x, axis=-1, eps=1e-05):
    m = jnp.mean(x, axis=axis, keepdims=True)
    v = jnp.var(x, axis=axis, keepdims=True)
    return (x - m) / jnp.sqrt(v + eps)

def _scatter_add(tgt, idx, src, axis=0):
    return tgt.at[idx].add(src)

def _segment_sum(src, seg, n):
    return jax.ops.segment_sum(src, seg, n)
kernel_name = 'mk_vit_tower_d1_tok_img4096_r4_020dea'

def setup_inputs(seed: int=0):
    np.random.seed(seed)
    _w = jnp.asarray

    def _rec_inputs():
        import jax
        import jax.numpy as jnp
        _rk = jax.random.key(seed)
        x = -0.0043416 + 0.998921 * jax.random.normal(jax.random.fold_in(_rk, 1), (32, 64, 64, 2), jnp.float32)
        return x
    x = _rec_inputs()

    def _L0_tok_setup():
        import jax, jax.numpy as jnp
        import numpy as np
        H, N, CH = (64, 64, 1)
        key = jax.random.key(seed)
        k1, k2, k3 = jax.random.split(key, 3)
        A_abslog = jnp.log(jax.random.uniform(k1, (H, N), dtype=jnp.float32, minval=0.5, maxval=0.999))
        A_phase = jax.random.uniform(k2, (H, N), dtype=jnp.float32, minval=-np.pi, maxval=np.pi)
        C = jax.random.normal(k3, (CH, H, N, 2), dtype=jnp.float32)
        return {'A_abslog': A_abslog, 'A_phase': A_phase, 'C': C, 'L': 1024}
    _L0_tok_all = _L0_tok_setup()
    _L0_tok_in = {k: v for k, v in _L0_tok_all.items() if k in ('A_abslog', 'A_phase')}
    del _L0_tok_all

    def _L0_attn_setup():
        import jax, jax.numpy as jnp
        import numpy as np
        NEG_INF = -1e+30

        def rotary_pos_emb(x):
            B, T, H, D = x.shape
            exponents = (jnp.arange(0, D, 2)[:D // 2] // D).astype(jnp.float32)
            freqs = 1.0 / jnp.power(jnp.float32(1000.0), exponents)
            theta = jnp.arange(T, dtype=jnp.float32)[:, None] * freqs[None, :]
            cos = jnp.cos(theta)[None, :, None, :]
            sin = jnp.sin(theta)[None, :, None, :]
            xr = x.astype(jnp.float32).reshape(B, T, H, D // 2, 2)
            x0, x1 = (xr[..., 0], xr[..., 1])
            out = jnp.stack([x0 * cos - x1 * sin, x0 * sin + x1 * cos], axis=-1)
            return out.reshape(B, T, H, D).astype(x.dtype)

        def attention_fwd(x, wq, wk, wv, wo, n_heads=32):
            B, T, C = x.shape
            hd = C // n_heads
            xq = (x @ wq.T).reshape(B, T, n_heads, hd)
            xk = (x @ wk.T).reshape(B, T, n_heads, hd)
            xv = (x @ wv.T).reshape(B, T, n_heads, hd)
            xq = rotary_pos_emb(xq)
            xk = rotary_pos_emb(xk)
            scale = hd ** (-0.5)
            scores = jnp.einsum('bqhd,bkhd->bhqk', xq, xk) * scale
            causal = jnp.tril(jnp.ones((T, T), dtype=bool))
            scores = jnp.where(causal[None, None], scores, NEG_INF)
            probs = jax.nn.softmax(scores.astype(jnp.float32), axis=-1).astype(xq.dtype)
            out = jnp.einsum('bhqk,bkhd->bqhd', probs, xv).reshape(B, T, C)
            return out @ wo.T
        key = jax.random.key(seed)
        ks = jax.random.split(key, 5)
        B, T, C = (2, 512, 1024)
        s = 0.02
        return {'x': jax.random.normal(ks[0], (B, T, C), jnp.float32), 'wq': jax.random.normal(ks[1], (C, C), jnp.float32) * s, 'wk': jax.random.normal(ks[2], (C, C), jnp.float32) * s, 'wv': jax.random.normal(ks[3], (C, C), jnp.float32) * s, 'wo': jax.random.normal(ks[4], (C, C), jnp.float32) * s}
    _L0_attn_all = _L0_attn_setup()
    _L0_attn_in = {k: v for k, v in _L0_attn_all.items() if k in ('wq', 'wk', 'wv', 'wo')}
    del _L0_attn_all

    def _L0_ffn_setup():
        import jax, jax.numpy as jnp
        import numpy as np
        B_L, B_H = (4, 8)
        LIN_SLOPE, LIN_INTER, EST_T = (1.0, 0.0, 64.0)
        BATCH, SEQ, IN_F, OUT_F = (4, 512, 1024, 1024)
        MAX_BITS = 8

        def dequant_kbit(qweight, lut, bit):
            O, I32 = (qweight.shape[1], qweight.shape[2])
            shifts = jnp.arange(32, dtype=jnp.int32)
            idx = jnp.zeros((O, I32 * 32), dtype=jnp.int32)
            for p in range(bit):
                bits = (qweight[p][:, :, None] >> shifts & 1).reshape(O, I32 * 32)
                idx = idx | bits << p
            return jnp.take_along_axis(lut, idx, axis=1)
        key = jax.random.key(seed)
        k = jax.random.split(key, 5)
        x = jax.random.normal(k[0], (BATCH, SEQ, IN_F), dtype=jnp.float32)
        qweight = jax.random.randint(k[1], (MAX_BITS, OUT_F, IN_F // 32), 0, 2147483647, dtype=jnp.int32)
        lut4 = jax.random.normal(k[2], (OUT_F, 2 ** B_L), dtype=jnp.float32) * 0.02
        lut8 = jax.random.normal(k[3], (OUT_F, 2 ** B_H), dtype=jnp.float32) * 0.02
        bias = jax.random.normal(k[4], (OUT_F,), dtype=jnp.float32) * 0.01
        return {'x': x, 'qweight': qweight, 'lut4': lut4, 'lut8': lut8, 'bias': bias}
    _L0_ffn_all = _L0_ffn_setup()
    _L0_ffn_in = {k: v for k, v in _L0_ffn_all.items() if k in ('qweight', 'lut4', 'lut8', 'bias')}
    del _L0_ffn_all
    return {'x': x, 'L0_tok_A_abslog': _L0_tok_in['A_abslog'], 'L0_tok_A_phase': _L0_tok_in['A_phase'], 'L0_attn_wq': _L0_attn_in['wq'], 'L0_attn_wk': _L0_attn_in['wk'], 'L0_attn_wv': _L0_attn_in['wv'], 'L0_attn_wo': _L0_attn_in['wo'], 'L0_ffn_qweight': _L0_ffn_in['qweight'], 'L0_ffn_lut4': _L0_ffn_in['lut4'], 'L0_ffn_lut8': _L0_ffn_in['lut8'], 'L0_ffn_bias': _L0_ffn_in['bias']}

def reference(x, L0_tok_A_abslog, L0_tok_A_phase, L0_attn_wq, L0_attn_wk, L0_attn_wv, L0_attn_wo, L0_ffn_qweight, L0_ffn_lut4, L0_ffn_lut8, L0_ffn_bias):
    import jax
    import jax.numpy as jnp

    def _L0_tok_ref(A_abslog, A_phase, C, L):
        import jax, jax.numpy as jnp
        import numpy as np
        H, N, CH = (64, 64, 1)
        A = jnp.exp(A_abslog + 1j * A_phase)
        dtA = jnp.log(A)
        Cc = C[..., 0] + 1j * C[..., 1]
        Cc = Cc * (A - 1.0) / dtA
        t = jnp.arange(L, dtype=jnp.float32)
        K = jnp.exp(dtA[:, :, None] * t)
        K = jnp.einsum('chn,hnl->chl', Cc, K)
        return 2.0 * K.real

    def _L0_attn_ref(x, wq, wk, wv, wo):
        import jax, jax.numpy as jnp
        import numpy as np
        NEG_INF = -1e+30

        def rotary_pos_emb(x):
            B, T, H, D = x.shape
            exponents = (jnp.arange(0, D, 2)[:D // 2] // D).astype(jnp.float32)
            freqs = 1.0 / jnp.power(jnp.float32(1000.0), exponents)
            theta = jnp.arange(T, dtype=jnp.float32)[:, None] * freqs[None, :]
            cos = jnp.cos(theta)[None, :, None, :]
            sin = jnp.sin(theta)[None, :, None, :]
            xr = x.astype(jnp.float32).reshape(B, T, H, D // 2, 2)
            x0, x1 = (xr[..., 0], xr[..., 1])
            out = jnp.stack([x0 * cos - x1 * sin, x0 * sin + x1 * cos], axis=-1)
            return out.reshape(B, T, H, D).astype(x.dtype)

        def attention_fwd(x, wq, wk, wv, wo, n_heads=32):
            B, T, C = x.shape
            hd = C // n_heads
            xq = (x @ wq.T).reshape(B, T, n_heads, hd)
            xk = (x @ wk.T).reshape(B, T, n_heads, hd)
            xv = (x @ wv.T).reshape(B, T, n_heads, hd)
            xq = rotary_pos_emb(xq)
            xk = rotary_pos_emb(xk)
            scale = hd ** (-0.5)
            scores = jnp.einsum('bqhd,bkhd->bhqk', xq, xk) * scale
            causal = jnp.tril(jnp.ones((T, T), dtype=bool))
            scores = jnp.where(causal[None, None], scores, NEG_INF)
            probs = jax.nn.softmax(scores.astype(jnp.float32), axis=-1).astype(xq.dtype)
            out = jnp.einsum('bhqk,bkhd->bqhd', probs, xv).reshape(B, T, C)
            return out @ wo.T
        return attention_fwd(x, wq, wk, wv, wo)

    def _L0_ffn_ref(x, qweight, lut4, lut8, bias):
        import jax, jax.numpy as jnp
        import numpy as np
        B_L, B_H = (4, 8)
        LIN_SLOPE, LIN_INTER, EST_T = (1.0, 0.0, 64.0)
        BATCH, SEQ, IN_F, OUT_F = (4, 512, 1024, 1024)
        MAX_BITS = 8

        def dequant_kbit(qweight, lut, bit):
            O, I32 = (qweight.shape[1], qweight.shape[2])
            shifts = jnp.arange(32, dtype=jnp.int32)
            idx = jnp.zeros((O, I32 * 32), dtype=jnp.int32)
            for p in range(bit):
                bits = (qweight[p][:, :, None] >> shifts & 1).reshape(O, I32 * 32)
                idx = idx | bits << p
            return jnp.take_along_axis(lut, idx, axis=1)
        e = jnp.linalg.norm(x, axis=-1) * LIN_SLOPE + LIN_INTER
        mask = e > EST_T
        w_l = dequant_kbit(qweight, lut4, B_L)
        w_h = dequant_kbit(qweight, lut8, B_H)
        y_l = jnp.einsum('bsi,oi->bso', x, w_l)
        y_h = jnp.einsum('bsi,oi->bso', x, w_h)
        y = jnp.where(mask[..., None], y_h, y_l) + bias
        return y
    h = _L0_tok_ref(L0_tok_A_abslog, L0_tok_A_phase, x, 1024)
    h = h + _L0_attn_ref(_layernorm(h, axis=-1), L0_attn_wq, L0_attn_wk, L0_attn_wv, L0_attn_wo)
    h = h + _L0_ffn_ref(_layernorm(h, axis=-1), L0_ffn_qweight, L0_ffn_lut4, L0_ffn_lut8, L0_ffn_bias)
    return h

_drawn_inputs = setup_inputs


def setup_inputs(seed=0):
    import zlib

    import numpy as np

    out = dict(_drawn_inputs(seed))
    spreads = {}
    factors = {'L0_ffn_bias': 7.349}
    for name, (base, spread) in spreads.items():
        noise = np.random.default_rng([zlib.crc32(name.encode()), seed]).standard_normal(out[name].shape)
        drawn = base * np.exp(spread * noise) if base else spread * noise
        out[name] = jnp.asarray(drawn.astype(out[name].dtype))
    for name, factor in factors.items():
        out[name] = (out[name] * factor).astype(out[name].dtype)
    return out
```

```python
from contextlib import ExitStack

import numpy as np

import concourse.bass as bass
import concourse.mybir as mybir

F32, F16, I32, U16 = mybir.dt.float32, mybir.dt.float16, mybir.dt.int32, mybir.dt.uint16
ALU, ACT, AX = mybir.AluOpType, mybir.ActivationFunctionType, mybir.AxisListType

P = 128
IMAGES, T, N = 32, 64, 64
L = 1024
TOKENS = IMAGES * T
TILES = TOKENS // P
IMGS = P // T
HEADS, HD = 32, 32
KT = L // P
HALF = 512
L1, L2, L3, L4 = 4, 256, 16, 16
HC = 4
CHUNKS = T // HC
PIECES = 4 * KT
PPC = PIECES // CHUNKS
XS, WS = 16.0, 64.0
PS = 256.0
EPS = 1e-5
MAGIC = 12582912.0
TWO_PI = 6.2831854820251465
UNDER_TWO_PI = 6.283185005187988
COLS = {"x1": (0, 16), "x2": (16, 16), "y1": (32, 16), "y2": (48, 16), "p1": (64, 4), "p2": (68, 4), "ar": (72, 1), "ai": (73, 1)}
J = 74
CH = 8
NCH = HEADS // CH
VW = HD + 1
LUT = 16
PLANES = 4
WORDS = 16
DQ_STEPS = 2 * L // P


def shape_constants():
    p = np.arange(P)
    t = p % T
    rows_im = p >= N
    cos, sin = np.cos(t.astype(np.float64)), np.sin(t.astype(np.float64))
    q_scale = XS / (XS * WS)
    rot = np.stack([cos * q_scale, sin * q_scale, -sin * q_scale], 1).astype(np.float32)
    mask = np.where(np.arange(T)[None, :] <= t[:, None], 0.0, -1e30).astype(np.float32)
    m = np.zeros(J)
    q = np.zeros((P, J))
    def put(name, mult, phase_re, phase_im):
        a, n = COLS[name]
        m[a:a + n] = mult
        q[:, a:a + n] = np.where(rows_im, phase_im, phase_re)[:, None]
    put("x1", 16.0 * np.arange(16), 0.25, 0.25)
    put("x2", 16.0 * np.arange(16), 0.5, 0.0)
    put("y1", np.arange(16), 0.25, 0.0)
    put("y2", np.arange(16), 0.0, 0.25)
    put("p1", 256.0 * np.arange(4), 0.25, 0.5)
    put("p2", 256.0 * np.arange(4), 0.5, 0.75)
    put("ar", 1.0, 0.25, 0.25)
    put("ai", 1.0, 0.0, 0.0)
    mults = np.broadcast_to(m, (P, J)).astype(np.float32)
    shifts = np.zeros((P, PLANES * 4 + PLANES * 4 + 8), np.int32)
    shifts[:, 0:16] = np.tile(np.arange(4), PLANES)
    shifts[:, 16:32] = np.repeat(np.arange(PLANES), 4)
    shifts[:, 32:40] = 4 * np.arange(8)
    return {"c_ident": np.eye(P, dtype=np.float32), "c_rot": rot, "c_mask": mask,
            "c_mults": np.ascontiguousarray(mults), "c_phase": q.astype(np.float32), "c_shifts": shifts}


def build(nc, a, out):
    ctx = ExitStack()
    with ctx:
        def sb(name, shape, dt):
            return ctx.enter_context(nc.sbuf_tensor("s_" + name, shape, dt))

        def sem(name):
            return ctx.enter_context(nc.semaphore(name))

        h0_dram = nc.dram_tensor("h0_scratch", (IMAGES, T, L), F32, kind="Internal").ap()
        h1_dram = nc.dram_tensor("h1_scratch", (TILES, P, L), F32, kind="Internal").ap()
        wf_dram = nc.dram_tensor("wf_scratch", (P, 4 * 2, DQ_STEPS, P), F16, kind="Internal").ap()
        h0_rows = h0_dram.rearrange("c h l -> (c h) l").rearrange("(n p) l -> n p l", p=P)

        weights = sb("weights", [P, PIECES, 2, L], F16)
        ident = sb("ident", [P, P], F32)
        rot_c = sb("rot_c", [P, 3], F32)
        mask = sb("mask", [P, T], F32)
        shifts = sb("shifts", [P, 40], I32)
        minus_half = sb("minus_half", [P, 1], F32)
        eps = sb("eps", [P, 1], F32)
        carrier = sb("carrier", [1, 2], F32)

        WORK = 20150
        work = sb("work", [P, WORK], F32)

        def carver():
            at = [0]

            def carve(dt, *shape):
                n = int(np.prod(shape))
                words = n if dt in (F32, I32) else (n + 1) // 2
                v = work[:, at[0]:at[0] + words]
                at[0] += words
                assert at[0] <= WORK, at[0]
                if dt != F32:
                    v = v.bitcast(dt)[:, 0:n]
                names = "abcd"[:len(shape)]
                if len(shape) > 1:
                    v = v.rearrange(f"p ({' '.join(names)}) -> p {' '.join(names)}", **dict(zip(names, shape)))
                return v
            return carve

        A = carver()
        w_stage = A(F32, 2, L)
        table = A(F32, T, J)
        abslog, phase = A(F32, T), A(F32, T)
        gr, gi, g_t1, g_t2, g_t3 = (A(F32, T) for _ in range(5))
        gp1, gp2, gp_t = (A(F32, T, L1) for _ in range(3))
        mults_s, phase_s = A(F32, J), A(F32, J)
        tab_start = A(F32, 1)
        A2 = carver()
        A2(F32, 2 * L + T * J + 7 * T + 3 * T * L1 + 2 * J + 1)
        ang, rnd = A2(F32, T, J), A2(F32, T, J)
        q_pow = A(F32, 2, HC, L2)
        q_tmp = A(F32, HC, L2)
        w_pow = A(F32, 2, HC, L1 * IMAGES)
        w_tmp = A(F32, HC, L1 * IMAGES)
        c_in = A(F32, 2, HC, 2, IMAGES)
        h0_stage = A(F32, 2, HC, L2)
        B = carver()
        h_in = B(F32, L)
        x_t = B(F16, 2, KT, P)
        scaled = B(F32, 2, HALF)
        rot = B(F32, L)
        q_t, k_t = B(F16, 2, KT, P), B(F16, 2, KT, P)
        q3, k3 = B(F16, HEADS, P), B(F16, HEADS, P)
        v_hi, v_lo = B(F16, HEADS, VW), B(F16, HEADS, VW)
        scores = B(F32, 2, CH, T)
        probs = B(F32, 2, CH, P)
        p_t = B(F16, 2, CH, P)
        o_n = B(F32, L)
        o_t = B(F16, 2, KT, P)
        h_res = B(F32, L)
        dq_words = B(I32, PLANES, WORDS)
        dq_lut = B(F32, LUT)
        dq_w = B(F32, HALF)
        dq_idx = B(U16, HALF)
        dq_planes = B(I32, WORDS * PLANES * 4)
        dq_mask = dq_planes.bitcast(U16)
        dq_planes = dq_planes.rearrange("p (w a) -> p w a", w=WORDS)
        dq_t = B(F16, 4, 2, P)
        stats = B(F32, 12)
        mv = B(F32, 2)
        rstd = B(F32, 2)
        mx = B(F32, 2, CH)
        inv = B(F32, CH)
        C = carver()
        assert C(F32, L) is not None
        hc = C(F32, 2, L)
        xc_t = C(F16, 2, 2, KT, P)
        bias = C(F32, L)
        statc = C(F32, 12)
        mvc = C(F32, 2)
        rstdc = C(F32, 2)
        hb = C(F32, 2, L)
        wf = weights[:, 0:KT, :, :].rearrange("p k s o -> p (k s o)").rearrange("p (k s t o) -> p k s t o", k=4, s=2, t=DQ_STEPS)

        banks = [ctx.enter_context(nc.psum_tensor(f"bank{i}", [P, HALF], F32)) for i in range(8)]
        G, M = banks[0:3], banks[3:7]
        out_bank = banks[7]

        S = {n: sem(n) for n in (
            "const_loaded ab_loaded c_loaded_0 c_loaded_1 w_loaded_0 w_loaded_1 table_step table_ang table_sin table_exp table_am gp_ready "
            "q_mult qt_mult q_ready w_mult wt_mult w_ready mixed h0_copied h0_stored_0 h0_stored_1 w_hi w_lo "
            "h_loaded ln_step var_ready rstd_ready xn_ready xt_pe xt_hi xt_lo "
            "q_pe q_scaled q_rotated qt_pe qt_hi qt_lo q_stacked k_pe k_scaled k_rotated kt_pe kt_hi kt_lo k_stacked "
            "v_pe v_hi_ready v_lo_ready s_pe s_masked s_max s_sub s_exp pt_pe pt_hi pt_lo av_pe av_inv o_ready "
            "ot_pe ot_hi ot_lo wo_pe h1_ready res_loaded h1_stored zeros_ready "
            "dq_loaded lut_loaded lut_ready dq_step dq_ready dqt_pe dqt_hi dqt_lo dq_stored "
            "wf_loaded eps_b eps_c carrier_ready bias_loaded hc_loaded_0 hc_loaded_1 cln_step cvar_ready crstd_ready cxn_ready cb_ready cxt_pe cxt_hi cxt_lo f_pe f_out out_stored_0 out_stored_1").split()}

        class Step:

            def __init__(self, engine, s, per_turn=0, turn=0):
                self.engine, self.s, self.per, self.turn, self.n = engine, s, per_turn, turn, 0

            def link(self, ins):
                self.n += 1
                ins.then_inc(self.s, 1)
                self.engine.wait_ge(self.s, self.turn * self.per + self.n)

        block = ctx.enter_context(nc.Block())

        def wait_ahead(s, count):
            nc.vector.wait_ge(s, count)
            nc.vector.tensor_copy(carrier[0:1, 1:2], carrier[0:1, 0:1])

        def col(name):
            s, n = COLS[name]
            return slice(s, s + n)

        @block.sync
        def _(sp):
            sp.dma_start(abslog[0:N], a["abslog_t"]).then_inc(S["ab_loaded"], 16)
            sp.dma_start(abslog[N:P], a["abslog_t"]).then_inc(S["ab_loaded"], 16)
            sp.dma_start(phase[0:N], a["phase_t"]).then_inc(S["ab_loaded"], 16)
            sp.dma_start(phase[N:P], a["phase_t"]).then_inc(S["ab_loaded"], 16)
            sp.dma_start(mults_s, a["c_mults"]).then_inc(S["ab_loaded"], 16)
            sp.dma_start(phase_s, a["c_phase"]).then_inc(S["ab_loaded"], 16)
            for dst, name in ((ident[:], "c_ident"), (rot_c[:], "c_rot"), (mask[:], "c_mask"), (shifts[:], "c_shifts")):
                sp.dma_start(dst, a[name]).then_inc(S["const_loaded"], 16)

            def mixer_chunk(g, par, first):
                n = 2 * g + par
                if not first:
                    sp.wait_ge(S["w_ready"], 2 * g + par - 1)
                elif par == 0:
                    sp.wait_ge(S["gp_ready"], 1)
                for half in range(2):
                    sp.dma_start(c_in[N * half:N * half + N, par], a["c_t"][n]).then_inc(S[f"c_loaded_{par}"], 16)
                for j in range(PPC):
                    if not first or j >= 2 or par:
                        sp.wait_ge(S["w_lo"], (2 * g + par) * PPC + j - 1)
                    sp.dma_start(w_stage[:, j % 2], a["w_t"][n * PPC + j]).then_inc(S[f"w_loaded_{j % 2}"], 16)

            def mixer_store(g, par):
                n = 2 * g + par
                sp.wait_ge(S["h0_copied"], 2 * n + 2)
                for l1 in range(L1):
                    sp.dma_start(h0_dram[:, bass.ds(n * HC, HC), l1 * L2:(l1 + 1) * L2],
                                 h0_stage[l1 * IMAGES:(l1 + 1) * IMAGES, par]).then_inc(S[f"h0_stored_{par}"], 16)

            mixer_chunk(0, 0, True)
            mixer_chunk(0, 1, True)
            with sp.Fori(1, CHUNKS // 2) as g:
                mixer_store(g - 1, 0)
                mixer_chunk(g, 0, False)
                mixer_store(g - 1, 1)
                mixer_chunk(g, 1, False)
            mixer_store(CHUNKS // 2 - 1, 0)
            mixer_store(CHUNKS // 2 - 1, 1)
            for par in range(2):
                sp.wait_ge(S[f"h0_stored_{par}"], 16 * L1 * CHUNKS // 2)
            sp.wait_ge(S["w_lo"], PIECES)

            def load_h(t):
                sp.dma_start(h_in, h0_rows[t]).then_inc(S["h_loaded"], 16)

            def stack(src, dst, order, t, stacked, s_hi, s_lo, drained):
                sp.wait_ge(S["s_pe"], 2 * NCH * t)
                sp.wait_ge(s_hi, 2 * t + 2)
                sp.wait_ge(s_lo, 2 * t + 2)
                for j in range(4):
                    for r, part in enumerate(order):
                        d = dst[32 * r:32 * r + 32].rearrange("p (k j) t -> p k j t", j=4)[:, :, j]
                        sp.dma_start(d, src[32 * j:32 * j + 32, part]).then_inc(stacked, 16)

            def turn(t, more, more_ln):
                if more_ln:
                    sp.wait_ge(S["xt_pe"], 2 * t + 4)
                    load_h(t + 2)
                sp.wait_ge(S["h1_stored"], 16 * t)
                sp.dma_start(h_res, h0_rows[t]).then_inc(S["res_loaded"], 16)
                sp.wait_ge(S["dq_ready"], t)
                sp.dma_start(dq_words, a["qwords"][t]).then_inc(S["dq_loaded"], 16)
                sp.dma_start(dq_lut, a["lut4_steps"][t]).then_inc(S["lut_loaded"], 16)
                if more:
                    stack(q_t, q3, (0, 1, 0), t + 1, S["q_stacked"], S["qt_hi"], S["qt_lo"], None)
                    stack(k_t, k3, (0, 0, 1), t + 1, S["k_stacked"], S["kt_hi"], S["kt_lo"], None)
                sp.wait_ge(S["dqt_lo"], t + 1)
                sp.dma_start(wf_dram[:, :, t, :], dq_t.rearrange("p k s o -> p (k s) o")).then_inc(S["dq_stored"], 16)
                sp.wait_ge(S["h1_ready"], 2 * t + 2)
                sp.dma_start(h1_dram[t], h_res).then_inc(S["h1_stored"], 16)

            load_h(0)
            sp.wait_ge(S["xt_pe"], 2)
            load_h(1)
            stack(q_t, q3, (0, 1, 0), 0, S["q_stacked"], S["qt_hi"], S["qt_lo"], None)
            stack(k_t, k3, (0, 0, 1), 0, S["k_stacked"], S["kt_hi"], S["kt_lo"], None)
            turn(0, True, True)
            with sp.Fori(1, TILES - 2) as t:
                turn(t, True, True)
            turn(TILES - 2, True, False)
            turn(TILES - 1, False, False)

            sp.wait_ge(S["dq_stored"], 16 * TILES)
            sp.wait_ge(S["v_pe"], 2 * TILES)
            for k in range(4):
                sp.dma_start(weights[:, 2 * k:2 * k + 2].rearrange("p k s o -> p (k s o)"),
                             wf_dram[:, 2 * k:2 * k + 2].rearrange("i k t o -> i (k t o)")).then_inc(S["wf_loaded"], 16)
            sp.wait_ge(S["h1_stored"], 16 * TILES)
            sp.dma_start(bias, a["bias_rows"]).then_inc(S["bias_loaded"], 16)

            def load_c(t, par):
                sp.dma_start(hc[:, par], h1_dram[t]).then_inc(S[f"hc_loaded_{par}"], 16)

            def store_c(t, par):
                sp.wait_ge(S["f_out"], 2 * t + 2)
                sp.dma_start(out[t], hb[:, par]).then_inc(S[f"out_stored_{par}"], 16)

            load_c(0, 0)
            load_c(1, 1)

            def pair(g, more):
                for par in range(2):
                    t = 2 * g + par
                    if more:
                        sp.wait_ge(S["cb_ready"], t + 1)
                        sp.wait_ge(S["cxt_pe"], 2 * t + 2)
                        load_c(t + 2, par)
                    store_c(t, par)
            pair(0, True)
            with sp.Fori(1, TILES // 2 - 1) as g:
                pair(g, True)
            pair(TILES // 2 - 1, False)
            for par in range(2):
                sp.wait_ge(S[f"out_stored_{par}"], 16 * TILES // 2)

        @block.tensor
        def _(pe):
            def mix(g, par):
                n = 2 * g + par
                pe.wait_ge(S["q_ready"], n + 1)
                pe.wait_ge(S["w_ready"], n + 1)
                pe.wait_ge(S["h0_copied"], 4 * g)
                for h in range(HC):
                    last = nc.tensor.matmul(banks[2 * par + h // 2][:, (h % 2) * L2:(h % 2 + 1) * L2],
                                            w_pow[:, par, h], q_pow[:, par, h], start=True, stop=True)
                    if h % 2:
                        last.then_inc(S["mixed"], 1)
            mix(0, 0)
            mix(0, 1)
            with pe.Fori(1, CHUNKS // 2) as g:
                mix(g, 0)
                mix(g, 1)

            def transpose8(src, b0, b1, done):
                for k in range(KT):
                    last = nc.tensor.transpose((b0 if k < 4 else b1)[:, (k % 4) * P:(k % 4 + 1) * P],
                                               src[:, k * P:(k + 1) * P], ident[:])
                    if k % 4 == 3:
                        last.then_inc(done, 1)

            def product(bank, x, w, half, done, part=(0, KT)):
                for k in range(*part):
                    for n, (xp, wp) in enumerate(((0, 0), (0, 1), (1, 0))):
                        last = nc.tensor.matmul(bank[:, :], x[:, xp, k], w(k, wp, half), start=(k == 0 and n == 0),
                                                stop=(k == KT - 1 and n == 2))
                if part[1] == KT:
                    last.then_inc(done, 1)

            def w_of(mat):
                return lambda k, part, half: weights[:, mat * KT + k, part, half * HALF:(half + 1) * HALF]

            FRONT, BACK = (0, KT // 2), (KT // 2, KT)
            Q, K, V, O = (w_of(m) for m in range(4))

            def x_transposes(t):
                pe.wait_ge(S["xn_ready"], t + 1)
                pe.wait_ge(S["kt_lo"], 2 * t)
                transpose8(h_in, M[2], M[3], S["xt_pe"])

            def body(t, att, qkv, ln):
                u = t + 1
                if qkv:
                    pe.wait_ge(S["xt_lo"], 2 * u + 2)
                    if att:
                        pe.wait_ge(S["h1_ready"], 2 * t)
                    product(G[0], x_t, Q, 0, S["q_pe"], FRONT)
                if att:
                    pe.wait_ge(S["q_stacked"], 16 * 12 * (t + 1))
                    pe.wait_ge(S["k_stacked"], 16 * 12 * (t + 1))

                def score_chunk(c):
                    for b in range(2):
                        if c:
                            pe.wait_ge(S["s_masked"], 16 * t + 4 * c - 2 + 2 * b)
                        for h in range(4):
                            head = c * CH + b * 4 + h
                            last = nc.tensor.matmul(M[b][:, h * P:(h + 1) * P], q3[0:96, head], k3[0:96, head],
                                                    start=True, stop=True)
                        last.then_inc(S["s_pe"], 1)

                def prob_transposes(c):
                    pe.wait_ge(S["s_exp"], 8 * t + 2 * c + 2)
                    for b in range(2):
                        if c:
                            pe.wait_ge(S["pt_lo"], 8 * t + 2 * c - 1 + b)
                        for h in range(4):
                            last = nc.tensor.transpose(M[2 + b][:, h * P:(h + 1) * P], probs[:, c % 2, b * 4 + h], ident[:])
                        last.then_inc(S["pt_pe"], 1)

                def values_chunk(c):
                    pe.wait_ge(S["pt_lo"], 8 * t + 2 * c + 2)
                    if c == 0:
                        pe.wait_ge(S["v_lo_ready"], 2 * t + 2)
                    if c >= 1:
                        pe.wait_ge(S["o_ready"], 4 * t + c)
                    for h in range(CH):
                        head = c * CH + h
                        o = out_bank[:, h * VW:(h + 1) * VW]
                        nc.tensor.matmul(o, p_t[:, 0, h], v_hi[:, head], start=True, stop=False)
                        nc.tensor.matmul(o, p_t[:, 0, h], v_lo[:, head], start=False, stop=False)
                        last = nc.tensor.matmul(o, p_t[:, 1, h], v_hi[:, head], start=False, stop=True)
                    last.then_inc(S["av_pe"], 1)

                if att:
                    pe.wait_ge(S["dqt_lo"], t)
                    score_chunk(0)
                    score_chunk(1)
                if qkv:
                    product(G[0], x_t, Q, 0, S["q_pe"], BACK)
                    product(G[1], x_t, Q, 1, S["q_pe"], FRONT)
                if att:
                    prob_transposes(0)
                    score_chunk(2)
                if qkv:
                    product(G[1], x_t, Q, 1, S["q_pe"], BACK)
                    product(G[2], x_t, K, 0, S["k_pe"], FRONT)
                if att:
                    values_chunk(0)
                    prob_transposes(1)
                    score_chunk(3)
                if qkv:
                    product(G[2], x_t, K, 0, S["k_pe"], BACK)
                    pe.wait_ge(S["q_rotated"], 4 * u + 4)
                    if att:
                        pe.wait_ge(S["s_masked"], 16 * t + 16)
                    transpose8(rot, M[0], M[1], S["qt_pe"])
                    product(G[0], x_t, K, 1, S["k_pe"], FRONT)
                if att:
                    values_chunk(1)
                    prob_transposes(2)
                if qkv:
                    product(G[0], x_t, K, 1, S["k_pe"], BACK)
                    product(G[1], x_t, V, 0, S["v_pe"], FRONT)
                if att:
                    values_chunk(2)
                    prob_transposes(3)
                if qkv:
                    product(G[1], x_t, V, 0, S["v_pe"], BACK)
                if att:
                    values_chunk(3)
                if qkv:
                    pe.wait_ge(S["k_rotated"], 4 * u + 4)
                    if att:
                        pe.wait_ge(S["pt_lo"], 8 * t + 8)
                    transpose8(rot, M[2], M[3], S["kt_pe"])
                    pe.wait_ge(S["k_rotated"], 4 * u + 2)
                    product(G[2], x_t, V, 1, S["v_pe"], FRONT)
                if att:
                    pe.wait_ge(S["o_ready"], 4 * t + 4)
                    if qkv:
                        pe.wait_ge(S["qt_lo"], 2 * u + 2)
                    transpose8(o_n, M[0], M[1], S["ot_pe"])
                if qkv:
                    product(G[2], x_t, V, 1, S["v_pe"], BACK)
                if ln:
                    x_transposes(t + 2)
                if att:
                    pe.wait_ge(S["ot_lo"], 2 * t + 2)
                    if qkv:
                        pe.wait_ge(S["k_rotated"], 4 * u + 4)
                        pe.wait_ge(S["v_lo_ready"], 2 * u + 1)
                    product(G[0], o_t, O, 0, S["wo_pe"])
                    product(G[1], o_t, O, 1, S["wo_pe"])
                    pe.wait_ge(S["dq_ready"], t + 1)
                    pe.wait_ge(S["ot_lo"], 2 * t + 2)
                    for k in range(4):
                        last = nc.tensor.transpose(M[0][:, k * P:(k + 1) * P], dq_w[:, k * P:(k + 1) * P], ident[:])
                    last.then_inc(S["dqt_pe"], 1)

            pe.wait_ge(S["xn_ready"], 1)
            pe.wait_ge(S["h0_copied"], 2 * CHUNKS)
            transpose8(h_in, M[2], M[3], S["xt_pe"])
            pe.wait_ge(S["xt_lo"], 2)
            pe.wait_ge(S["w_lo"], PIECES)
            body(-1, False, True, False)
            x_transposes(1)
            body(0, True, True, True)
            with pe.Fori(1, TILES - 2) as t:
                body(t, True, True, True)
            body(TILES - 2, True, True, False)
            body(TILES - 1, True, False, False)

            def wf_of(k, part, half):
                return wf[:, k % 4, part, :, :].rearrange("p (o h) c -> p o h c", h=2)[:, half * 4:half * 4 + 4, k // 4]

            def c_transposes(t, par, first=False):
                pe.wait_ge(S["cxn_ready"], t + 1)
                if first:
                    pe.wait_ge(S["dqt_lo"], TILES)
                else:
                    pe.wait_ge(S["cxt_lo"], 2 * t)
                transpose8(hc[:, par], M[0], M[1], S["cxt_pe"])

            def pair(g, more):
                for par in range(2):
                    t = 2 * g + par
                    pe.wait_ge(S["cxt_lo"], 2 * t + 2)
                    pe.wait_ge(S["f_out"], 2 * t)
                    product(G[1], xc_t[:, par], wf_of, 0, S["f_pe"])
                    if more or par == 0:
                        c_transposes(t + 1, 1 - par)
                    product(G[2], xc_t[:, par], wf_of, 1, S["f_pe"])
            c_transposes(0, 0, True)
            pe.wait_ge(S["wf_loaded"], 64)
            pe.wait_ge(S["h1_ready"], 2 * TILES)
            pair(0, True)
            with pe.Fori(1, TILES // 2 - 1) as g:
                pair(g, True)
            pair(TILES // 2 - 1, False)

        @block.scalar
        def _(act):
            act.wait_ge(S["table_ang"], 1)
            nc.scalar.activation(table, ang, ACT.Sin, scale=UNDER_TWO_PI).then_inc(S["table_sin"], 1)
            act.wait_ge(S["table_am"], 1)
            nc.scalar.activation(rnd, rnd, ACT.Exp).then_inc(S["table_exp"], 1)

            def chunk(g, par, first=False):
                n = 2 * g + par
                for j in range(PPC):
                    act.wait_ge(S[f"w_loaded_{j % 2}"], 16 * (n + 1))
                    nc.scalar.activation(weights[:, n * PPC + j, 0], w_stage[:, j % 2], ACT.Copy, scale=WS).then_inc(S["w_hi"], 1)
                for b in range(2):
                    act.wait_ge(S["mixed"], 2 * n + b + 1)
                    if not first:
                        act.wait_ge(S[f"h0_stored_{par}"], 16 * L1 * g)
                    nc.scalar.activation(h0_stage[:, par, 2 * b:2 * b + 2].rearrange("p h l -> p (h l)"),
                                         banks[2 * par + b][:, :], ACT.Copy).then_inc(S["h0_copied"], 1)
            chunk(0, 0, True)
            chunk(0, 1, True)
            with act.Fori(1, CHUNKS // 2) as g:
                chunk(g, 0)
                chunk(g, 1)

            def hi8(dst, b0, b1, ready, done, count, scale):
                for b, bank in enumerate((b0, b1)):
                    act.wait_ge(ready, count + b + 1)
                    nc.scalar.activation(dst[:, 0, 4 * b:4 * b + 4].rearrange("p k t -> p (k t)"), bank[:, :], ACT.Copy,
                                         scale=scale).then_inc(done, 1)

            def scale_half(u, half, bank, ready, done, previous, free):
                act.wait_ge(ready, 2 * u + half + 1)
                if previous is not None:
                    act.wait_ge(previous, free)
                nc.scalar.activation(scaled[:, half], bank[:, :], ACT.Copy, scale=rot_c[:, 0:1]).then_inc(done, 1)

            def values_half(u, half, bank):
                act.wait_ge(S["v_pe"], 2 * u + half + 1)
                act.wait_ge(S["av_pe"], NCH * u)
                nc.scalar.activation(v_hi[:, 16 * half:16 * half + 16, 0:HD], bank[:, :].rearrange("p (h d) -> p h d", d=HD),
                                     ACT.Copy, scale=XS / (XS * WS)).then_inc(S["v_hi_ready"], 1)

            def body(t, att, qkv, ln):
                u = t + 1

                def exps(c):
                    act.wait_ge(S["s_sub"], 4 * t + c + 1)
                    if c >= 2:
                        act.wait_ge(S["pt_pe"], 8 * t + 2 * c - 2)
                    else:
                        act.wait_ge(S["pt_pe"], 8 * t)
                    for i in range(IMGS):
                        r = slice(i * T, i * T + T)
                        nc.scalar.activation(probs[r, c % 2, :, i * T:i * T + T], scores[r, c % 2], ACT.Exp,
                                             scale=HD ** -0.5 / (XS * XS)).then_inc(S["s_exp"], 1)

                def p_hi(c):
                    for b in range(2):
                        act.wait_ge(S["pt_pe"], 8 * t + 2 * c + b + 1)
                        if b == 0:
                            act.wait_ge(S["av_pe"], 4 * t + c)
                        nc.scalar.activation(p_t[:, 0, 4 * b:4 * b + 4].rearrange("p k t -> p (k t)"), M[2 + b][:, :],
                                             ACT.Copy, scale=PS).then_inc(S["pt_hi"], 1)

                if att:
                    exps(0)
                if qkv:
                    scale_half(u, 0, G[0], S["q_pe"], S["q_scaled"], S["k_rotated"], 4 * u)
                if att:
                    exps(1)
                    p_hi(0)
                if qkv:
                    scale_half(u, 1, G[1], S["q_pe"], S["q_scaled"], None, 0)
                if att:
                    exps(2)
                    p_hi(1)
                    exps(3)
                if qkv:
                    act.wait_ge(S["q_stacked"], 16 * 12 * u)
                    hi8(q_t, M[0], M[1], S["qt_pe"], S["qt_hi"], 2 * u, 1.0)
                    scale_half(u, 0, G[2], S["k_pe"], S["k_scaled"], S["q_rotated"], 4 * u + 4)
                if att:
                    p_hi(2)
                if qkv:
                    scale_half(u, 1, G[0], S["k_pe"], S["k_scaled"], None, 0)
                if att:
                    p_hi(3)
                if qkv:
                    act.wait_ge(S["k_stacked"], 16 * 12 * u)
                    hi8(k_t, M[2], M[3], S["kt_pe"], S["kt_hi"], 2 * u, 1.0)
                    values_half(u, 0, G[1])
                if att:
                    act.wait_ge(S["wo_pe"], 2 * t)
                    hi8(o_t, M[0], M[1], S["ot_pe"], S["ot_hi"], 2 * t, 1.0)
                if qkv:
                    values_half(u, 1, G[2])
                if ln:
                    hi8(x_t, M[2], M[3], S["xt_pe"], S["xt_hi"], 2 * t + 4, XS)
                if att:
                    act.wait_ge(S["dqt_pe"], t + 1)
                    act.wait_ge(S["dq_stored"], 16 * t)
                    nc.scalar.activation(dq_t[:, :, 0], M[0][:, :].rearrange("p (k o) -> p k o", k=4), ACT.Copy,
                                         scale=WS).then_inc(S["dqt_hi"], 1)

            act.wait_ge(S["const_loaded"], 64)
            act.wait_ge(S["zeros_ready"], 1)
            hi8(x_t, M[2], M[3], S["xt_pe"], S["xt_hi"], 0, XS)
            body(-1, False, True, False)
            hi8(x_t, M[2], M[3], S["xt_pe"], S["xt_hi"], 2, XS)
            body(0, True, True, True)
            with act.Fori(1, TILES - 2) as t:
                body(t, True, True, True)
            body(TILES - 2, True, True, False)
            body(TILES - 1, True, False, False)

            def c_turn(t, par):
                act.wait_ge(S["f_pe"], 2 * t - 2) if not (isinstance(t, int) and t < 2) else None
                hi8(xc_t[:, par], M[0], M[1], S["cxt_pe"], S["cxt_hi"], 2 * t, XS)
            c_turn(0, 0)
            c_turn(1, 1)
            with act.Fori(1, TILES // 2) as g:
                for par in range(2):
                    c_turn(2 * g + par, par)

        @block.vector
        def _(dve):
            V = nc.vector
            st = Step(dve, S["table_step"])
            V.memset(minus_half[:], -0.5)
            V.memset(eps[:], EPS)
            V.memset(carrier[:], 0.0).then_inc(S["carrier_ready"], 1)
            dve.wait_ge(S["carrier_ready"], 1)
            dve.wait_ge(S["ab_loaded"], 96)
            ph_k, u_turn = g_t1, g_t2
            st.link(V.tensor_scalar(ph_k, phase, 1.0 / TWO_PI, MAGIC, ALU.mult, ALU.add))
            st.link(V.tensor_scalar(ph_k, ph_k, MAGIC, None, ALU.subtract))
            st.link(V.scalar_tensor_tensor(phase, ph_k, -TWO_PI, phase, ALU.mult, ALU.add))
            st.link(V.tensor_scalar(u_turn, phase, 1.0 / TWO_PI, None, ALU.mult))
            full = [P, T, J]
            st.link(V.tensor_tensor(ang, u_turn.unsqueeze(2).broadcast_to(full), mults_s.unsqueeze(1).broadcast_to(full), ALU.mult))
            st.link(V.tensor_scalar(rnd, ang, MAGIC, MAGIC, ALU.add, ALU.subtract))
            st.link(V.tensor_tensor(ang, ang, rnd, ALU.subtract))
            st.link(V.tensor_tensor(ang, ang, phase_s.unsqueeze(1).broadcast_to(full), ALU.add))
            st.link(V.tensor_scalar(rnd, ang, MAGIC, MAGIC, ALU.add, ALU.subtract))
            V.tensor_tensor(ang, ang, rnd, ALU.subtract).then_inc(S["table_ang"], 1)
            dve.wait_ge(S["table_ang"], 1)
            V.tensor_tensor(rnd, abslog.unsqueeze(2).broadcast_to(full), mults_s.unsqueeze(1).broadcast_to(full),
                            ALU.mult).then_inc(S["table_am"], 1)
            dve.wait_ge(S["table_sin"], 1)
            dve.wait_ge(S["table_exp"], 1)
            st.link(V.tensor_tensor(table, table, rnd, ALU.mult))
            ar, ai = table[:, :, col("ar")], table[:, :, col("ai")]
            a3 = lambda x: x.unsqueeze(2)
            st.link(V.tensor_scalar(ar, ar, 1.0, None, ALU.subtract))
            st.link(V.tensor_tensor(g_t1, abslog, abslog, ALU.mult))
            st.link(V.tensor_tensor(g_t2, phase, phase, ALU.mult))
            st.link(V.tensor_tensor(g_t1, g_t1, g_t2, ALU.add))
            st.link(V.reciprocal(g_t1, g_t1))
            st.link(V.tensor_tensor(a3(gr), ar, a3(abslog), ALU.mult))
            st.link(V.tensor_tensor(a3(g_t2), ai, a3(phase), ALU.mult))
            st.link(V.tensor_tensor(gr, gr, g_t2, ALU.add))
            st.link(V.tensor_tensor(a3(gi), ai, a3(abslog), ALU.mult))
            st.link(V.tensor_tensor(a3(g_t3), ar, a3(phase), ALU.mult))
            st.link(V.tensor_tensor(gi, gi, g_t3, ALU.subtract))
            st.link(V.tensor_tensor(gr, gr, g_t1, ALU.mult))
            st.link(V.tensor_tensor(gi, gi, g_t1, ALU.mult))
            st.link(V.tensor_scalar(gr, gr, 2.0, None, ALU.mult))
            st.link(V.tensor_scalar(gi, gi, 2.0, None, ALU.mult))
            s4 = [P, T, L1]
            p1, p2 = table[:, :, col("p1")], table[:, :, col("p2")]
            gr4, gi4 = a3(gr).broadcast_to(s4), a3(gi).broadcast_to(s4)
            st.link(V.tensor_tensor(gp1, p1, gr4, ALU.mult))
            st.link(V.tensor_tensor(gp_t, p2, gi4, ALU.mult))
            st.link(V.tensor_tensor(gp1, gp1, gp_t, ALU.add))
            st.link(V.tensor_tensor(gp2, p2, gr4, ALU.mult))
            st.link(V.tensor_tensor(gp_t, p1, gi4, ALU.mult))
            V.tensor_tensor(gp2, gp2, gp_t, ALU.subtract).then_inc(S["gp_ready"], 1)
            dve.wait_ge(S["gp_ready"], 1)

            def chunk(g, par, first=False):
                n = 2 * g + par
                hs = bass.ds(n * HC, HC)
                sq = [P, HC, L3, L4]
                q4 = q_pow[:, par].rearrange("p h (a b) -> p h a b", b=L4)
                if not first:
                    dve.wait_ge(S["mixed"], 2 * (n - 1))
                V.tensor_tensor(q4, table[:, hs, col("x1")].unsqueeze(3).broadcast_to(sq),
                                table[:, hs, col("y1")].unsqueeze(2).broadcast_to(sq), ALU.mult).then_inc(S["q_mult"], 1)
                dve.wait_ge(S[f"c_loaded_{par}"], 32 * (g + 1))
                sw = [P, HC, L1, IMAGES]
                w4 = w_pow[:, par].rearrange("p h (a b) -> p h a b", b=IMAGES)
                V.tensor_tensor(w4, c_in[:, par, :, 0].unsqueeze(2).broadcast_to(sw), gp1[:, hs].unsqueeze(3).broadcast_to(sw),
                                ALU.mult).then_inc(S["w_mult"], 1)
                dve.wait_ge(S["qt_mult"], n + 1)
                dve.wait_ge(S["q_mult"], n + 1)
                V.tensor_tensor(q_pow[:, par], q_pow[:, par], q_tmp, ALU.add).then_inc(S["q_ready"], 1)
                dve.wait_ge(S["wt_mult"], n + 1)
                dve.wait_ge(S["w_mult"], n + 1)
                V.tensor_tensor(w_pow[:, par], w_pow[:, par], w_tmp, ALU.add).then_inc(S["w_ready"], 1)
                for j in range(PPC):
                    dve.wait_ge(S["w_hi"], n * PPC + j + 1)
                    V.scalar_tensor_tensor(weights[:, n * PPC + j, 1], w_stage[:, j % 2], WS, weights[:, n * PPC + j, 0],
                                           ALU.mult, ALU.subtract).then_inc(S["w_lo"], 1)
            chunk(0, 0, True)
            chunk(0, 1, True)
            with dve.Fori(1, CHUNKS // 2) as g:
                chunk(g, 0)
                chunk(g, 1)

            def lo8(dst, b0, b1, ready, done, count, scale):
                for b, bank in enumerate((b0, b1)):
                    dve.wait_ge(ready, count + b + 1)
                    V.scalar_tensor_tensor(dst[:, 1, 4 * b:4 * b + 4].rearrange("p k t -> p (k t)"), bank[:, :], scale,
                                           dst[:, 0, 4 * b:4 * b + 4].rearrange("p k t -> p (k t)"), ALU.mult,
                                           ALU.subtract).then_inc(done, 1)

            def layer_norm(x, stat, mean_var, r, t, loaded, step, var, rs, xn):
                dve.wait_ge(*loaded)
                V.bn_stats(stat[:, 0:6], x[:, 0:HALF]).then_inc(step, 1)
                V.bn_stats(stat[:, 6:12], x[:, HALF:L]).then_inc(step, 1)
                wait_ahead(step, 2 * t + 2)
                V.bn_aggr(mean_var, stat).then_inc(var, 1)
                dve.wait_ge(rs, t + 1)
                return lambda: V.tensor_scalar(x, x, mean_var[:, 0:1], r[:, 1:2], ALU.subtract, ALU.mult).then_inc(xn, 1)

            def norm_b(t):
                layer_norm(h_in, stats, mv, rstd, t, (S["h_loaded"], 16 * t + 16), S["ln_step"], S["var_ready"], S["rstd_ready"], S["xn_ready"])()

            def rotate_half(u, half, bank, ready, free, done):
                dve.wait_ge(ready, 2 * u + half + 1)
                if free is not None:
                    dve.wait_ge(*free)
                b = bank[:, :].rearrange("p (d two) -> p two d", two=2)
                c = scaled[:, half].rearrange("p (d two) -> p two d", two=2)
                o = rot[:, half * HALF:(half + 1) * HALF].rearrange("p (d two) -> p two d", two=2)
                V.scalar_tensor_tensor(o[:, 0], b[:, 1], rot_c[:, 2:3], c[:, 0], ALU.mult, ALU.add).then_inc(done, 1)
                V.scalar_tensor_tensor(o[:, 1], b[:, 0], rot_c[:, 1:2], c[:, 1], ALU.mult, ALU.add).then_inc(done, 1)

            def values_half(u, half, bank):
                dve.wait_ge(S["v_hi_ready"], 2 * u + half + 1)
                hs = slice(16 * half, 16 * half + 16)
                V.scalar_tensor_tensor(v_lo[:, hs, 0:HD], bank[:, :].rearrange("p (h d) -> p h d", d=HD), XS / (XS * WS),
                                       v_hi[:, hs, 0:HD], ALU.mult, ALU.subtract).then_inc(S["v_lo_ready"], 1)

            DQ = 11 + 2 * LUT - 1

            def body(t, att, qkv, ln):
                u = t + 1
                dq = Step(dve, S["dq_step"], DQ, t)

                def masked(c):
                    for b in range(2):
                        dve.wait_ge(S["s_pe"], 8 * t + 2 * c + b + 1)
                        if b == 0:
                            dve.wait_ge(S["s_exp"], 8 * t + 2 * c - 2 if c >= 2 else 8 * t)
                        for i in range(IMGS):
                            r = slice(i * T, i * T + T)
                            src = M[b][r, :].rearrange("p (h s) -> p h s", h=4)[:, :, i * T:i * T + T]
                            V.tensor_tensor(scores[r, c % 2, 4 * b:4 * b + 4], src, mask[r, :].unsqueeze(1).broadcast_to([T, 4, T]),
                                            ALU.add).then_inc(S["s_masked"], 1)
                    dve.wait_ge(S["s_masked"], 16 * t + 4 * c + 4)
                    V.reduce_max(mx[:, c % 2], scores[:, c % 2], AX.X).then_inc(S["s_max"], 1)

                def p_lo(c):
                    for b in range(2):
                        dve.wait_ge(S["pt_hi"], 8 * t + 2 * c + b + 1)
                        V.scalar_tensor_tensor(p_t[:, 1, 4 * b:4 * b + 4].rearrange("p k t -> p (k t)"), M[2 + b][:, :], PS,
                                               p_t[:, 0, 4 * b:4 * b + 4].rearrange("p k t -> p (k t)"), ALU.mult,
                                               ALU.subtract).then_inc(S["pt_lo"], 1)

                def normalise(c):
                    dve.wait_ge(S["av_pe"], 4 * t + c + 1)
                    o = out_bank[:, 0:CH * VW].rearrange("p (h d) -> p h d", d=VW)
                    V.reciprocal(inv.unsqueeze(2), o[:, :, HD:VW]).then_inc(S["av_inv"], 1)
                    dve.wait_ge(S["av_inv"], 4 * t + c + 1)
                    if c == 0:
                        dve.wait_ge(S["ot_pe"], 2 * t)
                    V.tensor_tensor(o_n[:, c * CH * HD:(c + 1) * CH * HD].rearrange("p (h d) -> p h d", d=HD), o[:, :, 0:HD],
                                    inv.unsqueeze(2).broadcast_to([P, CH, HD]), ALU.mult).then_inc(S["o_ready"], 1)

                def dq_index():
                    dve.wait_ge(S["dq_loaded"], 16 * t + 16)
                    dve.wait_ge(S["lut_loaded"], 16 * t + 16)
                    dve.wait_ge(S["dqt_pe"], t)
                    d4 = dq_planes.rearrange("p w (a k) -> p w a k", a=PLANES)
                    s4 = [P, WORDS, 4]
                    for pl in range(PLANES):
                        V.tensor_tensor(d4[:, :, pl], dq_words[:, pl].unsqueeze(2).broadcast_to(s4),
                                        shifts[:, 4 * pl:4 * pl + 4].unsqueeze(1).broadcast_to(s4),
                                        ALU.logical_shift_right).then_inc(S["dq_step"], 1)
                    dq.n += PLANES
                    dve.wait_ge(S["dq_step"], t * DQ + dq.n)
                    dq.link(V.tensor_scalar(dq_planes, dq_planes, 0x11111111, None, ALU.bitwise_and))

                def dq_nibbles():
                    full = [P, WORDS, PLANES * 4]
                    dq.link(V.tensor_tensor(dq_planes, dq_planes, shifts[:, 16:32].unsqueeze(1).broadcast_to(full),
                                            ALU.logical_shift_left))
                    d4 = dq_planes.rearrange("p w (a k) -> p w a k", a=PLANES)
                    dq.link(V.tensor_tensor(d4[:, :, 0:2], d4[:, :, 0:2], d4[:, :, 2:4], ALU.bitwise_or))
                    dq.link(V.tensor_tensor(d4[:, :, 0], d4[:, :, 0], d4[:, :, 1], ALU.bitwise_or))
                    full = [P, WORDS, 8, 4]
                    codes = dq_w.bitcast(I32)
                    dq.link(V.tensor_tensor(codes.rearrange("p (w m k) -> p w m k", m=8, k=4),
                                            d4[:, :, 0].unsqueeze(2).broadcast_to(full),
                                            shifts[:, 32:40].unsqueeze(1).unsqueeze(3).broadcast_to(full),
                                            ALU.logical_shift_right))
                    dq.link(V.tensor_scalar(codes, codes, 15, None, ALU.bitwise_and))
                    dq.link(V.tensor_copy(dq_idx, codes))

                def dq_entries(a0, a1):
                    for v in range(a0, a1):
                        dq.link(V.tensor_scalar(dq_mask, dq_idx, float(v), None, ALU.is_equal))
                        if v == 0:
                            dq.link(V.tensor_scalar(dq_w, dq_mask, dq_lut[:, 0:1], None, ALU.mult))
                            continue
                        ins = V.scalar_tensor_tensor(dq_w, dq_mask, dq_lut[:, v:v + 1], dq_w, ALU.mult, ALU.add)
                        if v == LUT - 1:
                            ins.then_inc(S["dq_ready"], 1)
                        else:
                            dq.link(ins)
                    if a1 == LUT:
                        assert dq.n == DQ, dq.n

                if att:
                    masked(0)
                    masked(1)
                if qkv:
                    rotate_half(u, 0, G[0], S["q_scaled"], (S["kt_pe"], 2 * u), S["q_rotated"])
                if att:
                    dq_index()
                    p_lo(0)
                    masked(2)
                if qkv:
                    rotate_half(u, 1, G[1], S["q_scaled"], None, S["q_rotated"])
                if att:
                    dq_nibbles()
                    normalise(0)
                    p_lo(1)
                    masked(3)
                    dq_entries(0, 4)
                if qkv:
                    lo8(q_t, M[0], M[1], S["qt_hi"], S["qt_lo"], 2 * u, 1.0)
                    rotate_half(u, 0, G[2], S["k_scaled"], (S["qt_pe"], 2 * u + 2), S["k_rotated"])
                if att:
                    normalise(1)
                    p_lo(2)
                    dq_entries(4, 8)
                if qkv:
                    rotate_half(u, 1, G[0], S["k_scaled"], None, S["k_rotated"])
                if att:
                    normalise(2)
                    p_lo(3)
                    dq_entries(8, 12)
                    normalise(3)
                if qkv:
                    lo8(k_t, M[2], M[3], S["kt_hi"], S["kt_lo"], 2 * u, 1.0)
                    values_half(u, 0, G[1])
                if att:
                    lo8(o_t, M[0], M[1], S["ot_hi"], S["ot_lo"], 2 * t, 1.0)
                if ln:
                    norm_b(t + 2)
                if qkv:
                    values_half(u, 1, G[2])
                if ln:
                    lo8(x_t, M[2], M[3], S["xt_hi"], S["xt_lo"], 2 * t + 4, XS)
                if att:
                    dq_entries(12, 16)
                    dve.wait_ge(S["res_loaded"], 16 * t + 16)
                    for half, bank in enumerate((G[0], G[1])):
                        dve.wait_ge(S["wo_pe"], 2 * t + half + 1)
                        r = h_res[:, half * HALF:(half + 1) * HALF]
                        V.scalar_tensor_tensor(r, bank[:, :], 1.0 / (XS * WS), r, ALU.mult, ALU.add).then_inc(S["h1_ready"], 1)
                    dve.wait_ge(S["dqt_hi"], t + 1)
                    V.scalar_tensor_tensor(dq_t[:, :, 1], M[0][:, :].rearrange("p (k o) -> p k o", k=4), WS, dq_t[:, :, 0],
                                           ALU.mult, ALU.subtract).then_inc(S["dqt_lo"], 1)

            dve.wait_ge(S["const_loaded"], 64)
            norm_b(0)
            lo8(x_t, M[2], M[3], S["xt_hi"], S["xt_lo"], 0, XS)
            body(-1, False, True, False)
            norm_b(1)
            lo8(x_t, M[2], M[3], S["xt_hi"], S["xt_lo"], 2, XS)
            body(0, True, True, True)
            with dve.Fori(1, TILES - 2) as t:
                body(t, True, True, True)
            body(TILES - 2, True, True, False)
            body(TILES - 1, True, False, False)

            def norm_c(g, par):
                t = 2 * g + par
                f = layer_norm(hc[:, par], statc, mvc, rstdc, t, (S[f"hc_loaded_{par}"], 16 * g + 16), S["cln_step"], S["cvar_ready"], S["crstd_ready"], S["cxn_ready"])
                dve.wait_ge(S["cb_ready"], t + 1)
                f()

            def sums(t, par):
                for half, bank in enumerate((G[1], G[2])):
                    dve.wait_ge(S["f_pe"], 2 * t + half + 1)
                    r = hb[:, par, half * HALF:(half + 1) * HALF]
                    V.scalar_tensor_tensor(r, bank[:, :], 1.0 / (XS * WS), r, ALU.mult, ALU.add).then_inc(S["f_out"], 1)

            norm_c(0, 0)
            lo8(xc_t[:, 0], M[0], M[1], S["cxt_hi"], S["cxt_lo"], 0, XS)

            def pair(g, more):
                for par in range(2):
                    t = 2 * g + par
                    if more or par == 0:
                        norm_c(g + par, 1 - par)
                        lo8(xc_t[:, 1 - par], M[0], M[1], S["cxt_hi"], S["cxt_lo"], 2 * t + 2, XS)
                    sums(t, par)
            pair(0, True)
            with dve.Fori(1, TILES // 2 - 1) as g:
                pair(g, True)
            pair(TILES // 2 - 1, False)

        @block.gpsimd
        def _(pool):
            Gp = nc.gpsimd

            pool.wait_ge(S["gp_ready"], 1)

            def chunk(g, par, first=False):
                n = 2 * g + par
                hs = bass.ds(n * HC, HC)
                sq, sw = [P, HC, L3, L4], [P, HC, L1, IMAGES]
                if not (first and par == 0):
                    pool.wait_ge(S["q_ready"], n)
                Gp.tensor_tensor(q_tmp.rearrange("p h (a b) -> p h a b", b=L4), table[:, hs, col("x2")].unsqueeze(3).broadcast_to(sq),
                                 table[:, hs, col("y2")].unsqueeze(2).broadcast_to(sq), ALU.mult).then_inc(S["qt_mult"], 1)
                pool.wait_ge(S[f"c_loaded_{par}"], 32 * (g + 1))
                if not (first and par == 0):
                    pool.wait_ge(S["w_ready"], n)
                Gp.tensor_tensor(w_tmp.rearrange("p h (a b) -> p h a b", b=IMAGES), c_in[:, par, :, 1].unsqueeze(2).broadcast_to(sw),
                                 gp2[:, hs].unsqueeze(3).broadcast_to(sw), ALU.mult).then_inc(S["wt_mult"], 1)
            chunk(0, 0, True)
            chunk(0, 1, True)
            with pool.Fori(1, CHUNKS // 2) as g:
                chunk(g, 0)
                chunk(g, 1)

            for par in range(2):
                pool.wait_ge(S[f"h0_stored_{par}"], 16 * L1 * CHUNKS // 2)
            pool.wait_ge(S["w_lo"], PIECES)
            pool.wait_ge(S["w_ready"], CHUNKS)
            Gp.memset(probs, 0.0)
            Gp.memset(v_lo, 0.0)
            Gp.memset(v_hi[:, :, 0:HD], 0.0)
            Gp.memset(v_hi[:, :, HD:VW], 1.0).then_inc(S["zeros_ready"], 1)

            def inv_std(t, var, mean_var, r, done, step=None):
                pool.wait_ge(var, t + 1)
                Gp.tensor_tensor(r[:, 0:1], mean_var[:, 1:2], eps[:], ALU.add).then_inc(step, 1)
                pool.wait_ge(step, t + 1)
                Gp.tensor_tensor(r[:, 1:2], r[:, 0:1], minus_half[:], ALU.pow).then_inc(done, 1)

            eps_b, eps_c = S["eps_b"], S["eps_c"]

            def body(t, att, ln):
                if att:
                    for c in range(NCH):
                        pool.wait_ge(S["s_max"], 4 * t + c + 1)
                        Gp.tensor_tensor(scores[:, c % 2], scores[:, c % 2], mx[:, c % 2].unsqueeze(2).broadcast_to([P, CH, T]),
                                         ALU.subtract).then_inc(S["s_sub"], 1)
                if ln:
                    inv_std(t + 2, S["var_ready"], mv, rstd, S["rstd_ready"], eps_b)
            inv_std(0, S["var_ready"], mv, rstd, S["rstd_ready"], eps_b)
            inv_std(1, S["var_ready"], mv, rstd, S["rstd_ready"], eps_b)
            body(0, True, True)
            with pool.Fori(1, TILES - 2) as t:
                body(t, True, True)
            body(TILES - 2, True, False)
            body(TILES - 1, True, False)

            pool.wait_ge(S["bias_loaded"], 16)

            def c_turn(g, par, first=False):
                t = 2 * g + par
                pool.wait_ge(S[f"hc_loaded_{par}"], 16 * g + 16)
                if not first:
                    pool.wait_ge(S[f"out_stored_{par}"], 16 * g)
                Gp.tensor_tensor(hb[:, par], hc[:, par], bias, ALU.add).then_inc(S["cb_ready"], 1)
                inv_std(t, S["cvar_ready"], mvc, rstdc, S["crstd_ready"], eps_c)
            c_turn(0, 0, True)
            c_turn(0, 1, True)
            with pool.Fori(1, TILES // 2) as g:
                for par in range(2):
                    c_turn(g, par)


def kernel(x, L0_tok_A_abslog, L0_tok_A_phase, L0_attn_wq, L0_attn_wk, L0_attn_wv, L0_attn_wo, L0_ffn_qweight,
           L0_ffn_lut4, L0_ffn_lut8, L0_ffn_bias):
    import concourse.bacc as bacc
    from concourse.bass_utils import run_bass_kernel_spmd

    def lay(v):
        return np.ascontiguousarray(v)

    arrays = {
        "c_t": lay(np.asarray(x).transpose(2, 1, 3, 0).reshape(N, CHUNKS, HC, 2, IMAGES).transpose(1, 0, 2, 3, 4)),
        "abslog_t": lay(np.asarray(L0_tok_A_abslog).T),
        "phase_t": lay(np.asarray(L0_tok_A_phase).T),
        "w_t": lay(np.stack([np.asarray(w).T.reshape(KT, P, L) for w in (L0_attn_wq, L0_attn_wk, L0_attn_wv, L0_attn_wo)])
                   .reshape(PIECES, P, L)),
        "qwords": lay(np.asarray(L0_ffn_qweight)[0:PLANES].reshape(PLANES, L // P, P, 2, WORDS).transpose(1, 3, 2, 0, 4)
                      .reshape(DQ_STEPS, P, PLANES, WORDS)),
        "lut4_steps": lay(np.repeat(np.asarray(L0_ffn_lut4).reshape(L // P, P, LUT), 2, axis=0)),
        "bias_rows": lay(np.broadcast_to(np.asarray(L0_ffn_bias)[None, :], (P, L))),
        **shape_constants(),
    }
    nc = bacc.Bacc("TRN2", target_bir_lowering=False, num_devices=1)
    aps = {n: nc.dram_tensor("in_" + n, v.shape, mybir.dt.from_np(v.dtype), kind="ExternalInput").ap() for n, v in arrays.items()}
    out = nc.dram_tensor("out_h", (TILES, P, L), F32, kind="ExternalOutput").ap()
    build(nc, aps, out)
    r = run_bass_kernel_spmd(nc, [{"in_" + n: v for n, v in arrays.items()}], core_ids=[0])
    return r.results[0]["out_h"].reshape(IMAGES, T, L)
```

```python
from contextlib import ExitStack

import numpy as np

import concourse.bass as bass
import concourse.mybir as mybir

F32, F16, I32, U16 = mybir.dt.float32, mybir.dt.float16, mybir.dt.int32, mybir.dt.uint16
ALU, ACT, AX = mybir.AluOpType, mybir.ActivationFunctionType, mybir.AxisListType

P = 128
IMAGES, T, N = 32, 64, 64
L = 1024
TOKENS = IMAGES * T
TILES = TOKENS // P
IMGS = P // T
HEADS, HD = 32, 32
KT = L // P
HALF = 512
L1, L2, L3, L4 = 4, 256, 16, 16
HC = 4
CHUNKS = T // HC
PIECES = 4 * KT
PPC = PIECES // CHUNKS
XS, WS = 16.0, 64.0
PS = 256.0
EPS = 1e-5
MAGIC = 12582912.0
TWO_PI = 6.2831854820251465
UNDER_TWO_PI = 6.283185005187988
COLS = {"x1": (0, 16), "x2": (16, 16), "y1": (32, 16), "y2": (48, 16), "p1": (64, 4), "p2": (68, 4), "ar": (72, 1), "ai": (73, 1)}
J = 74
CH = 8
NCH = HEADS // CH
VW = HD + 1
LUT = 16
PLANES = 4
WORDS = 16
DQ_STEPS = 2 * L // P
TERMS = LUT - 1


def shape_constants():
    p = np.arange(P)
    t = p % T
    rows_im = p >= N
    cos, sin = np.cos(t.astype(np.float64)), np.sin(t.astype(np.float64))
    q_scale = XS / (XS * WS)
    rot = np.stack([cos * q_scale, sin * q_scale, -sin * q_scale], 1).astype(np.float32)
    mask = np.where(np.arange(T)[None, :] <= t[:, None], 0.0, -1e30).astype(np.float32)
    m = np.zeros(J)
    q = np.zeros((P, J))
    def put(name, mult, phase_re, phase_im):
        a, n = COLS[name]
        m[a:a + n] = mult
        q[:, a:a + n] = np.where(rows_im, phase_im, phase_re)[:, None]
    put("x1", 16.0 * np.arange(16), 0.25, 0.25)
    put("x2", 16.0 * np.arange(16), 0.5, 0.0)
    put("y1", np.arange(16), 0.25, 0.0)
    put("y2", np.arange(16), 0.0, 0.25)
    put("p1", 256.0 * np.arange(4), 0.25, 0.5)
    put("p2", 256.0 * np.arange(4), 0.5, 0.75)
    put("ar", 1.0, 0.25, 0.25)
    put("ai", 1.0, 0.0, 0.0)
    mults = np.broadcast_to(m, (P, J)).astype(np.float32)
    shifts = np.zeros((P, PLANES * 4 + PLANES * 4 + 8), np.int32)
    shifts[:, 0:16] = np.tile(np.arange(4), PLANES)
    shifts[:, 16:32] = np.repeat(np.arange(PLANES), 4)
    shifts[:, 32:40] = 4 * np.arange(8)
    return {"c_ident": np.eye(P, dtype=np.float32), "c_rot": rot, "c_mask": mask,
            "c_mults": np.ascontiguousarray(mults), "c_phase": q.astype(np.float32), "c_shifts": shifts}


def build(nc, a, out):
    ctx = ExitStack()
    with ctx:
        def sb(name, shape, dt):
            return ctx.enter_context(nc.sbuf_tensor("s_" + name, shape, dt))

        def sem(name):
            return ctx.enter_context(nc.semaphore(name))

        h0_dram = nc.dram_tensor("h0_scratch", (IMAGES, T, L), F32, kind="Internal").ap()
        h1_dram = nc.dram_tensor("h1_scratch", (TILES, P, L), F32, kind="Internal").ap()
        wf_dram = nc.dram_tensor("wf_scratch", (P, 4 * 2, DQ_STEPS, P), F16, kind="Internal").ap()
        h0_rows = h0_dram.rearrange("c h l -> (c h) l").rearrange("(n p) l -> n p l", p=P)

        weights = sb("weights", [P, PIECES, 2, L], F16)
        ident = sb("ident", [P, P], F32)
        rot_c = sb("rot_c", [P, 3], F32)
        mask = sb("mask", [P, T], F32)
        shifts = sb("shifts", [P, 40], I32)
        minus_half = sb("minus_half", [P, 1], F32)
        eps = sb("eps", [P, 1], F32)
        carrier = sb("carrier", [1, 2], F32)

        WORK = 20150
        work = sb("work", [P, WORK], F32)

        def carver():
            at = [0]

            def carve(dt, *shape):
                n = int(np.prod(shape))
                words = n if dt in (F32, I32) else (n + 1) // 2
                v = work[:, at[0]:at[0] + words]
                at[0] += words
                assert at[0] <= WORK, at[0]
                if dt != F32:
                    v = v.bitcast(dt)[:, 0:n]
                names = "abcd"[:len(shape)]
                if len(shape) > 1:
                    v = v.rearrange(f"p ({' '.join(names)}) -> p {' '.join(names)}", **dict(zip(names, shape)))
                return v
            return carve

        A = carver()
        w_stage = A(F32, 2, L)
        table = A(F32, T, J)
        abslog, phase = A(F32, T), A(F32, T)
        gr, gi, g_t1, g_t2, g_t3 = (A(F32, T) for _ in range(5))
        gp1, gp2, gp_t = (A(F32, T, L1) for _ in range(3))
        mults_s, phase_s = A(F32, J), A(F32, J)
        tab_start = A(F32, 1)
        A2 = carver()
        A2(F32, 2 * L + T * J + 7 * T + 3 * T * L1 + 2 * J + 1)
        ang, rnd = A2(F32, T, J), A2(F32, T, J)
        q_pow = A(F32, 2, HC, L2)
        q_tmp = A(F32, HC, L2)
        w_pow = A(F32, 2, HC, L1 * IMAGES)
        w_tmp = A(F32, HC, L1 * IMAGES)
        c_in = A(F32, 2, HC, 2, IMAGES)
        h0_stage = A(F32, 2, HC, L2)
        B = carver()
        h_in = B(F32, L)
        x_t = B(F16, 2, KT, P)
        q_t, k_t = B(F16, 2, KT, P), B(F16, 2, KT, P)
        q3, k3 = B(F16, HEADS, P), B(F16, HEADS, P)
        p_t = B(F16, 2, CH, P)
        rot = B(F32, L)
        h_res = rot
        v_hi, v_lo = B(F16, HEADS, VW), B(F16, HEADS, VW)
        scores = B(F32, 2, CH, T)
        probs = B(F32, 2, CH, P)
        o_n = B(F32, L)
        o_t = B(F16, 2, KT, P)
        dq_words = B(I32, PLANES, WORDS)
        dq_lut = B(F32, LUT)
        dq_w = B(F32, HALF)
        dq_term = B(F32, 2, HALF)
        dq_idx = B(U16, HALF)
        dq_mask = B(U16, 4, HALF)
        dq_planes = dq_mask[:, 3].bitcast(I32).rearrange("p (w a) -> p w a", w=WORDS)
        dq_t = B(F16, 4, 2, P)
        stats, statc = B(F32, 12), B(F32, 12)
        mv, mvc = B(F32, 2), B(F32, 2)
        rstd, rstdc = B(F32, 2), B(F32, 2)
        mx = B(F32, 2, CH)
        inv = B(F32, CH)
        C = carver()
        SLOTS = 4
        hc = C(F32, SLOTS, L)
        xc_t = C(F16, 2, 2, KT, P)
        xn = C(F32, 2, L)
        bias = C(F32, L)
        wf = weights[:, 0:KT, :, :].rearrange("p k s o -> p (k s o)").rearrange("p (k s t o) -> p k s t o", k=4, s=2, t=DQ_STEPS)

        banks = [ctx.enter_context(nc.psum_tensor(f"bank{i}", [P, HALF], F32)) for i in range(8)]
        G, M = banks[0:3], banks[3:7]
        out_bank = banks[7]

        S = {n: sem(n) for n in (
            "const_loaded ab_loaded c_loaded_0 c_loaded_1 w_loaded_0 w_loaded_1 table_step table_ang table_sin table_exp table_am gp_ready "
            "q_mult qt_mult q_ready w_mult wt_mult w_ready mixed h0_copied h0_stored_0 h0_stored_1 w_hi w_lo "
            "h_loaded dq_masked dq_termed dq_sum ln_step var_ready rstd_ready xn_ready xt_pe xt_hi xt_lo "
            "q_pe q_scaled q_rotated qt_pe qt_hi qt_lo q_stacked k_pe k_scaled k_rotated kt_pe kt_hi kt_lo k_stacked "
            "v_pe v_hi_ready v_lo_ready s_pe s_masked s_max s_sub s_exp pt_pe pt_hi pt_lo av_pe av_inv o_ready "
            "ot_pe ot_hi ot_lo wo_pe h1_ready res_loaded h1_stored zeros_ready "
            "dq_loaded lut_loaded lut_ready dq_step dqt_pe dqt_hi dqt_lo dq_stored "
            "wf_loaded eps_b eps_c carrier_ready bias_loaded hc_loaded_0 hc_loaded_1 hc_loaded_2 hc_loaded_3 cln_step cvar_ready crstd_ready cxn_ready cb_ready cxt_pe cxt_hi cxt_lo f_pe f_out out_stored_0 out_stored_1 out_stored_2 out_stored_3").split()}

        class Step:

            def __init__(self, engine, s, per_turn=0, turn=0):
                self.engine, self.s, self.per, self.turn, self.n = engine, s, per_turn, turn, 0

            def link(self, ins):
                self.n += 1
                ins.then_inc(self.s, 1)
                self.engine.wait_ge(self.s, self.turn * self.per + self.n)

        block = ctx.enter_context(nc.Block())

        def wait_ahead(s, count):
            nc.vector.wait_ge(s, count)
            nc.vector.tensor_copy(carrier[0:1, 1:2], carrier[0:1, 0:1])

        def col(name):
            s, n = COLS[name]
            return slice(s, s + n)

        @block.sync
        def _(sp):
            sp.dma_start(abslog[0:N], a["abslog_t"]).then_inc(S["ab_loaded"], 16)
            sp.dma_start(abslog[N:P], a["abslog_t"]).then_inc(S["ab_loaded"], 16)
            sp.dma_start(phase[0:N], a["phase_t"]).then_inc(S["ab_loaded"], 16)
            sp.dma_start(phase[N:P], a["phase_t"]).then_inc(S["ab_loaded"], 16)
            sp.dma_start(mults_s, a["c_mults"]).then_inc(S["ab_loaded"], 16)
            sp.dma_start(phase_s, a["c_phase"]).then_inc(S["ab_loaded"], 16)
            for dst, name in ((ident[:], "c_ident"), (rot_c[:], "c_rot"), (mask[:], "c_mask"), (shifts[:], "c_shifts")):
                sp.dma_start(dst, a[name]).then_inc(S["const_loaded"], 16)

            def mixer_chunk(g, par, first):
                n = 2 * g + par
                if not first:
                    sp.wait_ge(S["w_ready"], 2 * g + par - 1)
                elif par == 0:
                    sp.wait_ge(S["gp_ready"], 1)
                for half in range(2):
                    sp.dma_start(c_in[N * half:N * half + N, par], a["c_t"][n]).then_inc(S[f"c_loaded_{par}"], 16)
                for j in range(PPC):
                    if not first or j >= 2 or par:
                        sp.wait_ge(S["w_lo"], (2 * g + par) * PPC + j - 1)
                    sp.dma_start(w_stage[:, j % 2], a["w_t"][n * PPC + j]).then_inc(S[f"w_loaded_{j % 2}"], 16)

            def mixer_store(g, par):
                n = 2 * g + par
                sp.wait_ge(S["h0_copied"], 2 * n + 2)
                for l1 in range(L1):
                    sp.dma_start(h0_dram[:, bass.ds(n * HC, HC), l1 * L2:(l1 + 1) * L2],
                                 h0_stage[l1 * IMAGES:(l1 + 1) * IMAGES, par]).then_inc(S[f"h0_stored_{par}"], 16)

            mixer_chunk(0, 0, True)
            mixer_chunk(0, 1, True)
            with sp.Fori(1, CHUNKS // 2) as g:
                mixer_store(g - 1, 0)
                mixer_chunk(g, 0, False)
                mixer_store(g - 1, 1)
                mixer_chunk(g, 1, False)
            mixer_store(CHUNKS // 2 - 1, 0)
            mixer_store(CHUNKS // 2 - 1, 1)
            for par in range(2):
                sp.wait_ge(S[f"h0_stored_{par}"], 16 * L1 * CHUNKS // 2)
            sp.wait_ge(S["w_lo"], PIECES)

            def load_h(t):
                sp.dma_start(h_in, h0_rows[t]).then_inc(S["h_loaded"], 16)

            def stack(src, dst, order, t, stacked, s_hi, s_lo):
                sp.wait_ge(S["s_pe"], 2 * NCH * t)
                sp.wait_ge(s_hi, 2 * t + 2)
                sp.wait_ge(s_lo, 2 * t + 2)
                for j in range(4):
                    for r, part in enumerate(order):
                        d = dst[32 * r:32 * r + 32].rearrange("p (k j) t -> p k j t", j=4)[:, :, j]
                        sp.dma_start(d, src[32 * j:32 * j + 32, part]).then_inc(stacked, 16)

            def turn(t, more, more_ln):
                if more_ln:
                    sp.wait_ge(S["xt_pe"], 2 * t + 4)
                    load_h(t + 2)
                if not (isinstance(t, int) and t == 0):
                    sp.wait_ge(S["dq_sum"], TERMS * t)
                sp.dma_start(dq_words, a["qwords"][t]).then_inc(S["dq_loaded"], 16)
                sp.dma_start(dq_lut, a["lut4_steps"][t]).then_inc(S["lut_loaded"], 16)
                if more:
                    stack(q_t, q3, (0, 1, 0), t + 1, S["q_stacked"], S["qt_hi"], S["qt_lo"])
                    stack(k_t, k3, (0, 0, 1), t + 1, S["k_stacked"], S["kt_hi"], S["kt_lo"])
                    sp.wait_ge(S["kt_pe"], 2 * t + 4)
                else:
                    sp.wait_ge(S["h1_stored"], 16 * t)
                sp.dma_start(h_res, h0_rows[t]).then_inc(S["res_loaded"], 16)
                if not more:
                    prefetch_c()
                sp.wait_ge(S["dqt_lo"], t + 1)
                if more:
                    sp.dma_start(wf_dram[:, :, t, :], dq_t.rearrange("p k s o -> p (k s) o")).then_inc(S["dq_stored"], 16)
                else:
                    sp.dma_start(wf[:, :, :, t, :].rearrange("p k s o -> p (k s) o"),
                                 dq_t.rearrange("p k s o -> p (k s) o")).then_inc(S["wf_loaded"], 16)
                sp.wait_ge(S["h1_ready"], 2 * t + 2)
                sp.dma_start(h1_dram[t], h_res).then_inc(S["h1_stored"], 16)

            def load_c(t, slot):
                sp.dma_start(hc[:, slot], h1_dram[t]).then_inc(S[f"hc_loaded_{slot}"], 16)

            def prefetch_c():
                sp.wait_ge(S["v_pe"], 2 * TILES)
                sp.wait_ge(S["q_stacked"], 16 * 12 * TILES)
                sp.wait_ge(S["k_stacked"], 16 * 12 * TILES)
                for slot in range(SLOTS):
                    load_c(slot, slot)
                sp.wait_ge(S["dq_stored"], 16 * (DQ_STEPS - 1))
                for k in range(4):
                    sp.dma_start(wf[:, k, :, 0:DQ_STEPS - 1], wf_dram[:, 2 * k:2 * k + 2, 0:DQ_STEPS - 1]).then_inc(S["wf_loaded"], 16)
                sp.wait_ge(S["av_pe"], NCH * TILES)
                sp.dma_start(bias, a["bias_rows"]).then_inc(S["bias_loaded"], 16)

            load_h(0)
            sp.wait_ge(S["xt_pe"], 2)
            load_h(1)
            stack(q_t, q3, (0, 1, 0), 0, S["q_stacked"], S["qt_hi"], S["qt_lo"])
            stack(k_t, k3, (0, 0, 1), 0, S["k_stacked"], S["kt_hi"], S["kt_lo"])
            turn(0, True, True)
            with sp.Fori(1, TILES - 2) as t:
                turn(t, True, True)
            turn(TILES - 2, True, False)
            turn(TILES - 1, False, False)

            sp.wait_ge(S["h1_stored"], 16 * TILES)

            def four(g, first=False, last=False):
                for slot in range(SLOTS):
                    t = SLOTS * g + slot
                    sp.wait_ge(S["f_out"], 2 * t + 2)
                    sp.dma_start(out[t], hc[:, slot]).then_inc(S[f"out_stored_{slot}"], 16)
                    if slot and not last:
                        sp.wait_ge(S[f"out_stored_{slot - 1}"], 16 * g + 16)
                        load_c(t + 3, slot - 1)
                    elif not slot and not first:
                        sp.wait_ge(S[f"out_stored_{SLOTS - 1}"], 16 * g)
                        load_c(t + 3, SLOTS - 1)
            four(0, first=True)
            with sp.Fori(1, TILES // SLOTS - 1) as g:
                four(g)
            four(TILES // SLOTS - 1, last=True)
            for slot in range(SLOTS):
                sp.wait_ge(S[f"out_stored_{slot}"], 16 * TILES // SLOTS)

        @block.tensor
        def _(pe):
            def mix(g, par):
                n = 2 * g + par
                pe.wait_ge(S["q_ready"], n + 1)
                pe.wait_ge(S["w_ready"], n + 1)
                pe.wait_ge(S["h0_copied"], 4 * g)
                for h in range(HC):
                    last = nc.tensor.matmul(banks[2 * par + h // 2][:, (h % 2) * L2:(h % 2 + 1) * L2],
                                            w_pow[:, par, h], q_pow[:, par, h], start=True, stop=True)
                    if h % 2:
                        last.then_inc(S["mixed"], 1)
            mix(0, 0)
            mix(0, 1)
            with pe.Fori(1, CHUNKS // 2) as g:
                mix(g, 0)
                mix(g, 1)

            def transpose8(src, b0, b1, done):
                for k in range(KT):
                    last = nc.tensor.transpose((b0 if k < 4 else b1)[:, (k % 4) * P:(k % 4 + 1) * P],
                                               src[:, k * P:(k + 1) * P], ident[:])
                    if k % 4 == 3:
                        last.then_inc(done, 1)

            def product(bank, x, w, half, done, part=(0, KT)):
                for k in range(*part):
                    for n, (xp, wp) in enumerate(((0, 0), (0, 1), (1, 0))):
                        last = nc.tensor.matmul(bank[:, :], x[:, xp, k], w(k, wp, half), start=(k == 0 and n == 0),
                                                stop=(k == KT - 1 and n == 2))
                if part[1] == KT:
                    last.then_inc(done, 1)

            def w_of(mat):
                return lambda k, part, half: weights[:, mat * KT + k, part, half * HALF:(half + 1) * HALF]

            FRONT, BACK = (0, KT // 2), (KT // 2, KT)
            Q, K, V, O = (w_of(m) for m in range(4))

            def x_transposes(t):
                pe.wait_ge(S["xn_ready"], t + 1)
                pe.wait_ge(S["kt_lo"], 2 * t)
                transpose8(h_in, M[2], M[3], S["xt_pe"])

            def body(t, att, qkv, ln):
                u = t + 1
                if qkv:
                    pe.wait_ge(S["xt_lo"], 2 * u + 2)
                    if att and not (isinstance(t, int) and t == 0):
                        pe.wait_ge(S["h1_ready"], 2 * t - 1)
                    product(G[0], x_t, Q, 0, S["q_pe"], FRONT)
                if att:
                    pe.wait_ge(S["q_stacked"], 16 * 12 * (t + 1))
                    pe.wait_ge(S["k_stacked"], 16 * 12 * (t + 1))

                def score_chunk(c):
                    for b in range(2):
                        if c:
                            pe.wait_ge(S["s_masked"], 16 * t + 4 * c - 2 + 2 * b)
                        for h in range(4):
                            head = c * CH + b * 4 + h
                            last = nc.tensor.matmul(M[b][:, h * P:(h + 1) * P], q3[0:96, head], k3[0:96, head],
                                                    start=True, stop=True)
                        last.then_inc(S["s_pe"], 1)

                def prob_transposes(c):
                    pe.wait_ge(S["s_exp"], 8 * t + 2 * c + 2)
                    for b in range(2):
                        if c:
                            pe.wait_ge(S["pt_lo"], 8 * t + 2 * c - 1 + b)
                        for h in range(4):
                            last = nc.tensor.transpose(M[2 + b][:, h * P:(h + 1) * P], probs[:, c % 2, b * 4 + h], ident[:])
                        last.then_inc(S["pt_pe"], 1)

                def values_chunk(c):
                    pe.wait_ge(S["pt_lo"], 8 * t + 2 * c + 2)
                    if c == 0:
                        pe.wait_ge(S["v_lo_ready"], 2 * t + 2)
                    if c >= 1:
                        pe.wait_ge(S["o_ready"], 4 * t + c)
                    for h in range(CH):
                        head = c * CH + h
                        o = out_bank[:, h * VW:(h + 1) * VW]
                        nc.tensor.matmul(o, p_t[:, 0, h], v_hi[:, head], start=True, stop=False)
                        nc.tensor.matmul(o, p_t[:, 0, h], v_lo[:, head], start=False, stop=False)
                        last = nc.tensor.matmul(o, p_t[:, 1, h], v_hi[:, head], start=False, stop=True)
                    last.then_inc(S["av_pe"], 1)

                if att:
                    if not (isinstance(t, int) and t == 0):
                        pe.wait_ge(S["ot_lo"], 2 * t)
                    score_chunk(0)
                if qkv:
                    product(G[0], x_t, Q, 0, S["q_pe"], BACK)
                if att:
                    score_chunk(1)
                if qkv:
                    if att:
                        pe.wait_ge(S["h1_ready"], 2 * t)
                    product(G[1], x_t, Q, 1, S["q_pe"], FRONT)
                if att:
                    prob_transposes(0)
                    score_chunk(2)
                if qkv:
                    product(G[1], x_t, Q, 1, S["q_pe"], BACK)
                    product(G[2], x_t, K, 0, S["k_pe"], FRONT)
                if att:
                    pe.wait_ge(S["dqt_lo"], t)
                    values_chunk(0)
                    prob_transposes(1)
                    score_chunk(3)
                if qkv:
                    product(G[2], x_t, K, 0, S["k_pe"], BACK)
                    pe.wait_ge(S["q_rotated"], 4 * u + 4)
                    if att:
                        pe.wait_ge(S["s_masked"], 16 * t + 16)
                    transpose8(rot, M[0], M[1], S["qt_pe"])
                    product(G[0], x_t, K, 1, S["k_pe"], FRONT)
                if att:
                    values_chunk(1)
                    prob_transposes(2)
                if qkv:
                    product(G[0], x_t, K, 1, S["k_pe"], BACK)
                    product(G[1], x_t, V, 0, S["v_pe"], FRONT)
                if att:
                    values_chunk(2)
                    prob_transposes(3)
                if qkv:
                    product(G[1], x_t, V, 0, S["v_pe"], BACK)
                if att:
                    values_chunk(3)
                if qkv:
                    pe.wait_ge(S["k_rotated"], 4 * u + 4)
                    if att:
                        pe.wait_ge(S["pt_lo"], 8 * t + 8)
                    transpose8(rot, M[2], M[3], S["kt_pe"])
                    product(G[2], x_t, V, 1, S["v_pe"], FRONT)
                if att:
                    pe.wait_ge(S["o_ready"], 4 * t + 4)
                    if qkv:
                        pe.wait_ge(S["qt_lo"], 2 * u + 2)
                    transpose8(o_n, M[0], M[1], S["ot_pe"])
                if qkv:
                    product(G[2], x_t, V, 1, S["v_pe"], BACK)
                if ln:
                    x_transposes(t + 2)
                if att:
                    pe.wait_ge(S["dq_sum"], TERMS * (t + 1))
                    for k in range(4):
                        last = nc.tensor.transpose(out_bank[:, k * P:(k + 1) * P], dq_w[:, k * P:(k + 1) * P], ident[:])
                    last.then_inc(S["dqt_pe"], 1)
                    pe.wait_ge(S["ot_lo"], 2 * t + 2)
                    if qkv:
                        pe.wait_ge(S["v_lo_ready"], 2 * u + 1)
                    product(G[0], o_t, O, 0, S["wo_pe"])
                    product(G[1], o_t, O, 1, S["wo_pe"])

            pe.wait_ge(S["xn_ready"], 1)
            pe.wait_ge(S["h0_copied"], 2 * CHUNKS)
            transpose8(h_in, M[2], M[3], S["xt_pe"])
            pe.wait_ge(S["xt_lo"], 2)
            pe.wait_ge(S["w_lo"], PIECES)
            body(-1, False, True, False)
            x_transposes(1)
            body(0, True, True, True)
            with pe.Fori(1, TILES - 2) as t:
                body(t, True, True, True)
            body(TILES - 2, True, True, False)
            body(TILES - 1, True, False, False)

            def wf_of(k, part, half):
                return wf[:, k % 4, part, :, :].rearrange("p (o h) c -> p o h c", h=2)[:, half * 4:half * 4 + 4, k // 4]

            F_BANKS = ((G[0], G[1]), (G[2], M[2]))

            def c_transposes(t, par, wait=True):
                pe.wait_ge(S["cxn_ready"], t + 1)
                if wait:
                    pe.wait_ge(S["cxt_lo"], 2 * t)
                transpose8(xn[:, par], M[0], M[1], S["cxt_pe"])

            def pair(g, first=False, last=False):
                for par in range(2):
                    t = 2 * g + par
                    pe.wait_ge(S["cxt_lo"], 2 * t + 2)
                    if not first:
                        pe.wait_ge(S["f_out"], 2 * t - 2)
                    product(F_BANKS[par][0], xc_t[:, par], wf_of, 0, S["f_pe"])
                    if not last or par == 0:
                        c_transposes(t + 1, 1 - par)
                    product(F_BANKS[par][1], xc_t[:, par], wf_of, 1, S["f_pe"])
            c_transposes(0, 0, wait=False)
            pe.wait_ge(S["wf_loaded"], 16 * 5)
            pe.wait_ge(S["h1_ready"], 2 * TILES)
            pair(0, first=True)
            with pe.Fori(1, TILES // 2 - 1) as g:
                pair(g)
            pair(TILES // 2 - 1, last=True)

        @block.scalar
        def _(act):
            act.wait_ge(S["table_ang"], 1)
            nc.scalar.activation(table, ang, ACT.Sin, scale=UNDER_TWO_PI).then_inc(S["table_sin"], 1)
            act.wait_ge(S["table_am"], 1)
            nc.scalar.activation(rnd, rnd, ACT.Exp).then_inc(S["table_exp"], 1)

            def chunk(g, par, first=False):
                n = 2 * g + par
                for j in range(PPC):
                    act.wait_ge(S[f"w_loaded_{j % 2}"], 16 * (n + 1))
                    nc.scalar.activation(weights[:, n * PPC + j, 0], w_stage[:, j % 2], ACT.Copy, scale=WS).then_inc(S["w_hi"], 1)
                for b in range(2):
                    act.wait_ge(S["mixed"], 2 * n + b + 1)
                    if not first:
                        act.wait_ge(S[f"h0_stored_{par}"], 16 * L1 * g)
                    nc.scalar.activation(h0_stage[:, par, 2 * b:2 * b + 2].rearrange("p h l -> p (h l)"),
                                         banks[2 * par + b][:, :], ACT.Copy).then_inc(S["h0_copied"], 1)
            chunk(0, 0, True)
            chunk(0, 1, True)
            with act.Fori(1, CHUNKS // 2) as g:
                chunk(g, 0)
                chunk(g, 1)

            def hi8(dst, b0, b1, ready, done, count, scale):
                for b, bank in enumerate((b0, b1)):
                    act.wait_ge(ready, count + b + 1)
                    nc.scalar.activation(dst[:, 0, 4 * b:4 * b + 4].rearrange("p k t -> p (k t)"), bank[:, :], ACT.Copy,
                                         scale=scale).then_inc(done, 1)

            def scale_half(u, half, bank, ready, done):
                act.wait_ge(ready, 2 * u + half + 1)
                nc.scalar.activation(rot[:, half * HALF:(half + 1) * HALF], bank[:, :], ACT.Copy, scale=rot_c[:, 0:1]).then_inc(done, 1)

            def values_half(u, half, bank):
                act.wait_ge(S["v_pe"], 2 * u + half + 1)
                act.wait_ge(S["av_pe"], NCH * u)
                nc.scalar.activation(v_hi[:, 16 * half:16 * half + 16, 0:HD], bank[:, :].rearrange("p (h d) -> p h d", d=HD),
                                     ACT.Copy, scale=XS / (XS * WS)).then_inc(S["v_hi_ready"], 1)

            def body(t, att, qkv, ln):
                u = t + 1

                def exps(c):
                    act.wait_ge(S["s_sub"], 4 * t + c + 1)
                    if c >= 2:
                        act.wait_ge(S["pt_pe"], 8 * t + 2 * c - 2)
                    else:
                        act.wait_ge(S["pt_pe"], 8 * t)
                    for i in range(IMGS):
                        r = slice(i * T, i * T + T)
                        nc.scalar.activation(probs[r, c % 2, :, i * T:i * T + T], scores[r, c % 2], ACT.Exp,
                                             scale=HD ** -0.5 / (XS * XS)).then_inc(S["s_exp"], 1)

                def p_hi(c):
                    for b in range(2):
                        act.wait_ge(S["pt_pe"], 8 * t + 2 * c + b + 1)
                        if b == 0:
                            act.wait_ge(S["av_pe"], 4 * t + c)
                        nc.scalar.activation(p_t[:, 0, 4 * b:4 * b + 4].rearrange("p k t -> p (k t)"), M[2 + b][:, :],
                                             ACT.Copy, scale=PS).then_inc(S["pt_hi"], 1)

                def dq_terms(v0, v1):
                    if v0 == 0:
                        act.wait_ge(S["lut_loaded"], 16 * t + 16)
                    for v in range(v0, v1):
                        act.wait_ge(S["dq_masked"], LUT * t + v + 1)
                        if v and not (isinstance(t, int) and TERMS * t + v <= 2):
                            act.wait_ge(S["dq_sum"], TERMS * t + max(v - 2, 0))
                        nc.scalar.activation(dq_term[:, v % 2] if v else dq_w, dq_mask[:, v % 4], ACT.Copy,
                                             scale=dq_lut[:, v:v + 1]).then_inc(S["dq_termed"], 1)

                if att:
                    exps(0)
                if qkv:
                    act.wait_ge(S["kt_pe"], 2 * u)
                    if att:
                        act.wait_ge(S["h1_stored"], 16 * t)
                    scale_half(u, 0, G[0], S["q_pe"], S["q_scaled"])
                if att:
                    p_hi(0)
                    exps(1)
                    dq_terms(0, 2)
                if qkv:
                    scale_half(u, 1, G[1], S["q_pe"], S["q_scaled"])
                if att:
                    p_hi(1)
                    dq_terms(2, 4)
                    exps(2)
                    exps(3)
                    dq_terms(4, 6)
                if qkv:
                    act.wait_ge(S["q_stacked"], 16 * 12 * u)
                    hi8(q_t, M[0], M[1], S["qt_pe"], S["qt_hi"], 2 * u, 1.0)
                    scale_half(u, 0, G[2], S["k_pe"], S["k_scaled"])
                if att:
                    dq_terms(6, 8)
                    p_hi(2)
                    dq_terms(8, 10)
                if qkv:
                    scale_half(u, 1, G[0], S["k_pe"], S["k_scaled"])
                if att:
                    p_hi(3)
                    dq_terms(10, 12)
                if qkv:
                    act.wait_ge(S["k_stacked"], 16 * 12 * u)
                    hi8(k_t, M[2], M[3], S["kt_pe"], S["kt_hi"], 2 * u, 1.0)
                    values_half(u, 0, G[1])
                if att:
                    dq_terms(12, 14)
                    act.wait_ge(S["wo_pe"], 2 * t)
                    hi8(o_t, M[0], M[1], S["ot_pe"], S["ot_hi"], 2 * t, 1.0)
                    dq_terms(14, 16)
                if qkv:
                    values_half(u, 1, G[2])
                if ln:
                    hi8(x_t, M[2], M[3], S["xt_pe"], S["xt_hi"], 2 * t + 4, XS)
                if att:
                    act.wait_ge(S["dqt_pe"], t + 1)
                    act.wait_ge(S["dq_stored"], 16 * t)
                    nc.scalar.activation(dq_t[:, :, 0], out_bank[:, :].rearrange("p (k o) -> p k o", k=4), ACT.Copy,
                                         scale=WS).then_inc(S["dqt_hi"], 1)

            act.wait_ge(S["const_loaded"], 64)
            act.wait_ge(S["zeros_ready"], 1)
            hi8(x_t, M[2], M[3], S["xt_pe"], S["xt_hi"], 0, XS)
            body(-1, False, True, False)
            hi8(x_t, M[2], M[3], S["xt_pe"], S["xt_hi"], 2, XS)
            body(0, True, True, True)
            with act.Fori(1, TILES - 2) as t:
                body(t, True, True, True)
            body(TILES - 2, True, True, False)
            body(TILES - 1, True, False, False)

            def c_turn(t, par):
                act.wait_ge(S["f_pe"], 2 * t - 2) if not (isinstance(t, int) and t < 2) else None
                hi8(xc_t[:, par], M[0], M[1], S["cxt_pe"], S["cxt_hi"], 2 * t, XS)
            c_turn(0, 0)
            c_turn(1, 1)
            with act.Fori(1, TILES // 2) as g:
                for par in range(2):
                    c_turn(2 * g + par, par)

        @block.vector
        def _(dve):
            V = nc.vector
            st = Step(dve, S["table_step"])
            V.memset(minus_half[:], -0.5)
            V.memset(eps[:], EPS)
            V.memset(carrier[:], 0.0).then_inc(S["carrier_ready"], 1)
            dve.wait_ge(S["carrier_ready"], 1)
            dve.wait_ge(S["ab_loaded"], 96)
            ph_k, u_turn = g_t1, g_t2
            st.link(V.tensor_scalar(ph_k, phase, 1.0 / TWO_PI, MAGIC, ALU.mult, ALU.add))
            st.link(V.tensor_scalar(ph_k, ph_k, MAGIC, None, ALU.subtract))
            st.link(V.scalar_tensor_tensor(phase, ph_k, -TWO_PI, phase, ALU.mult, ALU.add))
            st.link(V.tensor_scalar(u_turn, phase, 1.0 / TWO_PI, None, ALU.mult))
            full = [P, T, J]
            st.link(V.tensor_tensor(ang, u_turn.unsqueeze(2).broadcast_to(full), mults_s.unsqueeze(1).broadcast_to(full), ALU.mult))
            st.link(V.tensor_scalar(rnd, ang, MAGIC, MAGIC, ALU.add, ALU.subtract))
            st.link(V.tensor_tensor(ang, ang, rnd, ALU.subtract))
            st.link(V.tensor_tensor(ang, ang, phase_s.unsqueeze(1).broadcast_to(full), ALU.add))
            st.link(V.tensor_scalar(rnd, ang, MAGIC, MAGIC, ALU.add, ALU.subtract))
            V.tensor_tensor(ang, ang, rnd, ALU.subtract).then_inc(S["table_ang"], 1)
            dve.wait_ge(S["table_ang"], 1)
            V.tensor_tensor(rnd, abslog.unsqueeze(2).broadcast_to(full), mults_s.unsqueeze(1).broadcast_to(full),
                            ALU.mult).then_inc(S["table_am"], 1)
            dve.wait_ge(S["table_sin"], 1)
            dve.wait_ge(S["table_exp"], 1)
            st.link(V.tensor_tensor(table, table, rnd, ALU.mult))
            ar, ai = table[:, :, col("ar")], table[:, :, col("ai")]
            a3 = lambda x: x.unsqueeze(2)
            st.link(V.tensor_scalar(ar, ar, 1.0, None, ALU.subtract))
            st.link(V.tensor_tensor(g_t1, abslog, abslog, ALU.mult))
            st.link(V.tensor_tensor(g_t2, phase, phase, ALU.mult))
            st.link(V.tensor_tensor(g_t1, g_t1, g_t2, ALU.add))
            st.link(V.reciprocal(g_t1, g_t1))
            st.link(V.tensor_tensor(a3(gr), ar, a3(abslog), ALU.mult))
            st.link(V.tensor_tensor(a3(g_t2), ai, a3(phase), ALU.mult))
            st.link(V.tensor_tensor(gr, gr, g_t2, ALU.add))
            st.link(V.tensor_tensor(a3(gi), ai, a3(abslog), ALU.mult))
            st.link(V.tensor_tensor(a3(g_t3), ar, a3(phase), ALU.mult))
            st.link(V.tensor_tensor(gi, gi, g_t3, ALU.subtract))
            st.link(V.tensor_tensor(gr, gr, g_t1, ALU.mult))
            st.link(V.tensor_tensor(gi, gi, g_t1, ALU.mult))
            st.link(V.tensor_scalar(gr, gr, 2.0, None, ALU.mult))
            st.link(V.tensor_scalar(gi, gi, 2.0, None, ALU.mult))
            s4 = [P, T, L1]
            p1, p2 = table[:, :, col("p1")], table[:, :, col("p2")]
            gr4, gi4 = a3(gr).broadcast_to(s4), a3(gi).broadcast_to(s4)
            st.link(V.tensor_tensor(gp1, p1, gr4, ALU.mult))
            st.link(V.tensor_tensor(gp_t, p2, gi4, ALU.mult))
            st.link(V.tensor_tensor(gp1, gp1, gp_t, ALU.add))
            st.link(V.tensor_tensor(gp2, p2, gr4, ALU.mult))
            st.link(V.tensor_tensor(gp_t, p1, gi4, ALU.mult))
            V.tensor_tensor(gp2, gp2, gp_t, ALU.subtract).then_inc(S["gp_ready"], 1)
            dve.wait_ge(S["gp_ready"], 1)

            def chunk(g, par, first=False):
                n = 2 * g + par
                hs = bass.ds(n * HC, HC)
                sq = [P, HC, L3, L4]
                q4 = q_pow[:, par].rearrange("p h (a b) -> p h a b", b=L4)
                if not first:
                    dve.wait_ge(S["mixed"], 2 * (n - 1))
                V.tensor_tensor(q4, table[:, hs, col("x1")].unsqueeze(3).broadcast_to(sq),
                                table[:, hs, col("y1")].unsqueeze(2).broadcast_to(sq), ALU.mult).then_inc(S["q_mult"], 1)
                dve.wait_ge(S[f"c_loaded_{par}"], 32 * (g + 1))
                sw = [P, HC, L1, IMAGES]
                w4 = w_pow[:, par].rearrange("p h (a b) -> p h a b", b=IMAGES)
                V.tensor_tensor(w4, c_in[:, par, :, 0].unsqueeze(2).broadcast_to(sw), gp1[:, hs].unsqueeze(3).broadcast_to(sw),
                                ALU.mult).then_inc(S["w_mult"], 1)
                dve.wait_ge(S["qt_mult"], n + 1)
                dve.wait_ge(S["q_mult"], n + 1)
                V.tensor_tensor(q_pow[:, par], q_pow[:, par], q_tmp, ALU.add).then_inc(S["q_ready"], 1)
                dve.wait_ge(S["wt_mult"], n + 1)
                dve.wait_ge(S["w_mult"], n + 1)
                V.tensor_tensor(w_pow[:, par], w_pow[:, par], w_tmp, ALU.add).then_inc(S["w_ready"], 1)
                for j in range(PPC):
                    dve.wait_ge(S["w_hi"], n * PPC + j + 1)
                    V.scalar_tensor_tensor(weights[:, n * PPC + j, 1], w_stage[:, j % 2], WS, weights[:, n * PPC + j, 0],
                                           ALU.mult, ALU.subtract).then_inc(S["w_lo"], 1)
            chunk(0, 0, True)
            chunk(0, 1, True)
            with dve.Fori(1, CHUNKS // 2) as g:
                chunk(g, 0)
                chunk(g, 1)

            def lo8(dst, b0, b1, ready, done, count, scale):
                for b, bank in enumerate((b0, b1)):
                    dve.wait_ge(ready, count + b + 1)
                    V.scalar_tensor_tensor(dst[:, 1, 4 * b:4 * b + 4].rearrange("p k t -> p (k t)"), bank[:, :], scale,
                                           dst[:, 0, 4 * b:4 * b + 4].rearrange("p k t -> p (k t)"), ALU.mult,
                                           ALU.subtract).then_inc(done, 1)

            def norm_stats(x, stat, mean_var, t, loaded, step, var):
                dve.wait_ge(*loaded)
                V.bn_stats(stat[:, 0:6], x[:, 0:HALF]).then_inc(step, 1)
                V.bn_stats(stat[:, 6:12], x[:, HALF:L]).then_inc(step, 1)
                wait_ahead(step, 2 * t + 2)
                V.bn_aggr(mean_var, stat).then_inc(var, 1)

            def norm_stats_b(t):
                norm_stats(h_in, stats, mv, t, (S["h_loaded"], 16 * t + 16), S["ln_step"], S["var_ready"])

            def norm_b(t):
                dve.wait_ge(S["rstd_ready"], t + 1)
                V.tensor_scalar(h_in, h_in, mv[:, 0:1], rstd[:, 1:2], ALU.subtract, ALU.mult).then_inc(S["xn_ready"], 1)

            def rotate_half(u, half, bank, ready, done):
                dve.wait_ge(ready, 2 * u + half + 1)
                b = bank[:, :].rearrange("p (d two) -> p two d", two=2)
                o = rot[:, half * HALF:(half + 1) * HALF].rearrange("p (d two) -> p two d", two=2)
                V.scalar_tensor_tensor(o[:, 0], b[:, 1], rot_c[:, 2:3], o[:, 0], ALU.mult, ALU.add).then_inc(done, 1)
                V.scalar_tensor_tensor(o[:, 1], b[:, 0], rot_c[:, 1:2], o[:, 1], ALU.mult, ALU.add).then_inc(done, 1)

            def values_half(u, half, bank):
                dve.wait_ge(S["v_hi_ready"], 2 * u + half + 1)
                hs = slice(16 * half, 16 * half + 16)
                V.scalar_tensor_tensor(v_lo[:, hs, 0:HD], bank[:, :].rearrange("p (h d) -> p h d", d=HD), XS / (XS * WS),
                                       v_hi[:, hs, 0:HD], ALU.mult, ALU.subtract).then_inc(S["v_lo_ready"], 1)

            DQ = PLANES + 7

            def body(t, att, qkv, ln):
                u = t + 1
                dq = Step(dve, S["dq_step"], DQ, t)

                def masked(c):
                    for b in range(2):
                        dve.wait_ge(S["s_pe"], 8 * t + 2 * c + b + 1)
                        if b == 0:
                            dve.wait_ge(S["s_exp"], 8 * t + 2 * c - 2 if c >= 2 else 8 * t)
                        for i in range(IMGS):
                            r = slice(i * T, i * T + T)
                            src = M[b][r, :].rearrange("p (h s) -> p h s", h=4)[:, :, i * T:i * T + T]
                            V.tensor_tensor(scores[r, c % 2, 4 * b:4 * b + 4], src, mask[r, :].unsqueeze(1).broadcast_to([T, 4, T]),
                                            ALU.add).then_inc(S["s_masked"], 1)
                    dve.wait_ge(S["s_masked"], 16 * t + 4 * c + 4)
                    V.reduce_max(mx[:, c % 2], scores[:, c % 2], AX.X).then_inc(S["s_max"], 1)

                def p_lo(c):
                    for b in range(2):
                        dve.wait_ge(S["pt_hi"], 8 * t + 2 * c + b + 1)
                        V.scalar_tensor_tensor(p_t[:, 1, 4 * b:4 * b + 4].rearrange("p k t -> p (k t)"), M[2 + b][:, :], PS,
                                               p_t[:, 0, 4 * b:4 * b + 4].rearrange("p k t -> p (k t)"), ALU.mult,
                                               ALU.subtract).then_inc(S["pt_lo"], 1)

                def normalise(c):
                    dve.wait_ge(S["av_pe"], 4 * t + c + 1)
                    o = out_bank[:, 0:CH * VW].rearrange("p (h d) -> p h d", d=VW)
                    V.reciprocal(inv.unsqueeze(2), o[:, :, HD:VW]).then_inc(S["av_inv"], 1)
                    dve.wait_ge(S["av_inv"], 4 * t + c + 1)
                    if c == 0:
                        dve.wait_ge(S["ot_pe"], 2 * t)
                    V.tensor_tensor(o_n[:, c * CH * HD:(c + 1) * CH * HD].rearrange("p (h d) -> p h d", d=HD), o[:, :, 0:HD],
                                    inv.unsqueeze(2).broadcast_to([P, CH, HD]), ALU.mult).then_inc(S["o_ready"], 1)

                def dq_index():
                    dve.wait_ge(S["dq_loaded"], 16 * t + 16)
                    dve.wait_ge(S["dqt_pe"], t)
                    dve.wait_ge(S["dq_termed"], LUT * t)
                    d4 = dq_planes.rearrange("p w (a k) -> p w a k", a=PLANES)
                    s4 = [P, WORDS, 4]
                    for pl in range(PLANES):
                        V.tensor_tensor(d4[:, :, pl], dq_words[:, pl].unsqueeze(2).broadcast_to(s4),
                                        shifts[:, 4 * pl:4 * pl + 4].unsqueeze(1).broadcast_to(s4),
                                        ALU.logical_shift_right).then_inc(S["dq_step"], 1)
                    dq.n += PLANES
                    dve.wait_ge(S["dq_step"], t * DQ + dq.n)
                    dq.link(V.tensor_scalar(dq_planes, dq_planes, 0x11111111, None, ALU.bitwise_and))

                def dq_nibbles():
                    full = [P, WORDS, PLANES * 4]
                    dq.link(V.tensor_tensor(dq_planes, dq_planes, shifts[:, 16:32].unsqueeze(1).broadcast_to(full),
                                            ALU.logical_shift_left))
                    d4 = dq_planes.rearrange("p w (a k) -> p w a k", a=PLANES)
                    dq.link(V.tensor_tensor(d4[:, :, 0:2], d4[:, :, 0:2], d4[:, :, 2:4], ALU.bitwise_or))
                    dq.link(V.tensor_tensor(d4[:, :, 0], d4[:, :, 0], d4[:, :, 1], ALU.bitwise_or))
                    full = [P, WORDS, 8, 4]
                    codes = dq_w.bitcast(I32)
                    dq.link(V.tensor_tensor(codes.rearrange("p (w m k) -> p w m k", m=8, k=4),
                                            d4[:, :, 0].unsqueeze(2).broadcast_to(full),
                                            shifts[:, 32:40].unsqueeze(1).unsqueeze(3).broadcast_to(full),
                                            ALU.logical_shift_right))
                    dq.link(V.tensor_scalar(codes, codes, 15, None, ALU.bitwise_and))
                    dq.link(V.tensor_copy(dq_idx, codes))

                def dq_masks(v0, v1):
                    if v0:
                        dve.wait_ge(S["dq_termed"], LUT * t + v0)
                    for v in range(v0, v1):
                        V.tensor_scalar(dq_mask[:, v % 4], dq_idx, float(v), None, ALU.is_equal).then_inc(S["dq_masked"], 1)

                if att:
                    masked(0)
                    dq_index()
                    masked(1)
                if qkv:
                    rotate_half(u, 0, G[0], S["q_scaled"], S["q_rotated"])
                if att:
                    dq_nibbles()
                    dq_masks(0, 4)
                    p_lo(0)
                    masked(2)
                if qkv:
                    rotate_half(u, 1, G[1], S["q_scaled"], S["q_rotated"])
                if att:
                    normalise(0)
                    masked(3)
                    p_lo(1)
                if ln:
                    norm_stats_b(t + 2)
                if att:
                    dq_masks(4, 8)
                if qkv:
                    lo8(q_t, M[0], M[1], S["qt_hi"], S["qt_lo"], 2 * u, 1.0)
                    rotate_half(u, 0, G[2], S["k_scaled"], S["k_rotated"])
                if att:
                    normalise(1)
                    p_lo(2)
                if ln:
                    norm_b(t + 2)
                if att:
                    dq_masks(8, 12)
                if qkv:
                    rotate_half(u, 1, G[0], S["k_scaled"], S["k_rotated"])
                if att:
                    normalise(2)
                    p_lo(3)
                    dq_masks(12, 16)
                    normalise(3)
                if qkv:
                    lo8(k_t, M[2], M[3], S["kt_hi"], S["kt_lo"], 2 * u, 1.0)
                    values_half(u, 0, G[1])
                if att:
                    lo8(o_t, M[0], M[1], S["ot_hi"], S["ot_lo"], 2 * t, 1.0)
                if qkv:
                    values_half(u, 1, G[2])
                if ln:
                    lo8(x_t, M[2], M[3], S["xt_hi"], S["xt_lo"], 2 * t + 4, XS)
                if att:
                    dve.wait_ge(S["dqt_hi"], t + 1)
                    V.scalar_tensor_tensor(dq_t[:, :, 1], out_bank[:, :].rearrange("p (k o) -> p k o", k=4), WS, dq_t[:, :, 0],
                                           ALU.mult, ALU.subtract).then_inc(S["dqt_lo"], 1)
                    dve.wait_ge(S["res_loaded"], 16 * t + 16)
                    for half, bank in enumerate((G[0], G[1])):
                        dve.wait_ge(S["wo_pe"], 2 * t + half + 1)
                        r = h_res[:, half * HALF:(half + 1) * HALF]
                        V.scalar_tensor_tensor(r, bank[:, :], 1.0 / (XS * WS), r, ALU.mult, ALU.add).then_inc(S["h1_ready"], 1)

            dve.wait_ge(S["const_loaded"], 64)
            norm_stats_b(0)
            norm_b(0)
            lo8(x_t, M[2], M[3], S["xt_hi"], S["xt_lo"], 0, XS)
            norm_stats_b(1)
            norm_b(1)
            body(-1, False, True, False)
            lo8(x_t, M[2], M[3], S["xt_hi"], S["xt_lo"], 2, XS)
            body(0, True, True, True)
            with dve.Fori(1, TILES - 2) as t:
                body(t, True, True, True)
            body(TILES - 2, True, True, False)
            body(TILES - 1, True, False, False)

            def norm_c(t, g, slot, first=False):
                if not first:
                    dve.wait_ge(S["cxt_pe"], 2 * t - 2)
                norm_stats(hc[:, slot], statc, mvc, t, (S[f"hc_loaded_{slot}"], 16 * g + 16), S["cln_step"], S["cvar_ready"])
                dve.wait_ge(S["crstd_ready"], t + 1)
                V.tensor_scalar(xn[:, slot % 2], hc[:, slot], mvc[:, 0:1], rstdc[:, 1:2], ALU.subtract,
                                ALU.mult).then_inc(S["cxn_ready"], 1)
                dve.wait_ge(S["cxn_ready"], t + 1)
                V.tensor_tensor(hc[:, slot], hc[:, slot], bias, ALU.add).then_inc(S["cb_ready"], 1)

            def sum_half(t, slot, half):
                if half == 0:
                    dve.wait_ge(S["cb_ready"], t + 1)
                dve.wait_ge(S["f_pe"], 2 * t + half + 1)
                r = hc[:, slot, half * HALF:(half + 1) * HALF]
                bank = ((G[0], G[1]), (G[2], M[2]))[slot % 2][half]
                V.scalar_tensor_tensor(r, bank[:, :], 1.0 / (XS * WS), r, ALU.mult, ALU.add).then_inc(S["f_out"], 1)

            dve.wait_ge(S["bias_loaded"], 16)
            norm_c(0, 0, 0, True)
            norm_c(1, 0, 1, True)
            lo8(xc_t[:, 0], M[0], M[1], S["cxt_hi"], S["cxt_lo"], 0, XS)

            def four(g, last=False):
                for slot in range(SLOTS):
                    t = SLOTS * g + slot
                    sum_half(t, slot, 0)
                    if not last or slot < SLOTS - 1:
                        lo8(xc_t[:, 1 - slot % 2], M[0], M[1], S["cxt_hi"], S["cxt_lo"], 2 * t + 2, XS)
                    if not last or slot < SLOTS - 2:
                        norm_c(t + 2, g + (slot + 2) // SLOTS, (slot + 2) % SLOTS)
                    sum_half(t, slot, 1)
            with dve.Fori(0, TILES // SLOTS - 1) as g:
                four(g)
            four(TILES // SLOTS - 1, last=True)

        @block.gpsimd
        def _(pool):
            Gp = nc.gpsimd

            pool.wait_ge(S["gp_ready"], 1)

            def chunk(g, par, first=False):
                n = 2 * g + par
                hs = bass.ds(n * HC, HC)
                sq, sw = [P, HC, L3, L4], [P, HC, L1, IMAGES]
                if not (first and par == 0):
                    pool.wait_ge(S["q_ready"], n)
                Gp.tensor_tensor(q_tmp.rearrange("p h (a b) -> p h a b", b=L4), table[:, hs, col("x2")].unsqueeze(3).broadcast_to(sq),
                                 table[:, hs, col("y2")].unsqueeze(2).broadcast_to(sq), ALU.mult).then_inc(S["qt_mult"], 1)
                pool.wait_ge(S[f"c_loaded_{par}"], 32 * (g + 1))
                if not (first and par == 0):
                    pool.wait_ge(S["w_ready"], n)
                Gp.tensor_tensor(w_tmp.rearrange("p h (a b) -> p h a b", b=IMAGES), c_in[:, par, :, 1].unsqueeze(2).broadcast_to(sw),
                                 gp2[:, hs].unsqueeze(3).broadcast_to(sw), ALU.mult).then_inc(S["wt_mult"], 1)
            chunk(0, 0, True)
            chunk(0, 1, True)
            with pool.Fori(1, CHUNKS // 2) as g:
                chunk(g, 0)
                chunk(g, 1)

            for par in range(2):
                pool.wait_ge(S[f"h0_stored_{par}"], 16 * L1 * CHUNKS // 2)
            pool.wait_ge(S["w_lo"], PIECES)
            pool.wait_ge(S["w_ready"], CHUNKS)
            Gp.memset(probs, 0.0)
            Gp.memset(v_lo, 0.0)
            Gp.memset(v_hi[:, :, 0:HD], 0.0)
            Gp.memset(v_hi[:, :, HD:VW], 1.0).then_inc(S["zeros_ready"], 1)

            def inv_std(t, var, mean_var, r, done, step=None):
                pool.wait_ge(var, t + 1)
                Gp.tensor_tensor(r[:, 0:1], mean_var[:, 1:2], eps[:], ALU.add).then_inc(step, 1)
                pool.wait_ge(step, t + 1)
                Gp.tensor_tensor(r[:, 1:2], r[:, 0:1], minus_half[:], ALU.pow).then_inc(done, 1)

            eps_b, eps_c = S["eps_b"], S["eps_c"]

            def body(t, att, ln):
                def dq_adds(v0, v1):
                    for v in range(v0, v1):
                        pool.wait_ge(S["dq_termed"], LUT * t + v + 1)
                        if v > 1:
                            pool.wait_ge(S["dq_sum"], TERMS * t + v - 1)
                        Gp.tensor_tensor(dq_w, dq_w, dq_term[:, v % 2], ALU.add).then_inc(S["dq_sum"], 1)

                def less_max(c):
                    pool.wait_ge(S["s_max"], 4 * t + c + 1)
                    Gp.tensor_tensor(scores[:, c % 2], scores[:, c % 2], mx[:, c % 2].unsqueeze(2).broadcast_to([P, CH, T]),
                                     ALU.subtract).then_inc(S["s_sub"], 1)

                if att:
                    less_max(0)
                    less_max(1)
                    dq_adds(1, 2)
                    less_max(2)
                    dq_adds(2, 4)
                    less_max(3)
                if ln:
                    inv_std(t + 2, S["var_ready"], mv, rstd, S["rstd_ready"], eps_b)
                if att:
                    dq_adds(4, LUT)
            inv_std(0, S["var_ready"], mv, rstd, S["rstd_ready"], eps_b)
            inv_std(1, S["var_ready"], mv, rstd, S["rstd_ready"], eps_b)
            body(0, True, True)
            with pool.Fori(1, TILES - 2) as t:
                body(t, True, True)
            body(TILES - 2, True, False)
            body(TILES - 1, True, False)

            inv_std(0, S["cvar_ready"], mvc, rstdc, S["crstd_ready"], eps_c)
            with pool.Fori(1, TILES) as t:
                inv_std(t, S["cvar_ready"], mvc, rstdc, S["crstd_ready"], eps_c)


def kernel(x, L0_tok_A_abslog, L0_tok_A_phase, L0_attn_wq, L0_attn_wk, L0_attn_wv, L0_attn_wo, L0_ffn_qweight,
           L0_ffn_lut4, L0_ffn_lut8, L0_ffn_bias):
    import concourse.bacc as bacc
    from concourse.bass_utils import run_bass_kernel_spmd

    def lay(v):
        return np.ascontiguousarray(v)

    arrays = {
        "c_t": lay(np.asarray(x).transpose(2, 1, 3, 0).reshape(N, CHUNKS, HC, 2, IMAGES).transpose(1, 0, 2, 3, 4)),
        "abslog_t": lay(np.asarray(L0_tok_A_abslog).T),
        "phase_t": lay(np.asarray(L0_tok_A_phase).T),
        "w_t": lay(np.stack([np.asarray(w).T.reshape(KT, P, L) for w in (L0_attn_wq, L0_attn_wk, L0_attn_wv, L0_attn_wo)])
                   .reshape(PIECES, P, L)),
        "qwords": lay(np.asarray(L0_ffn_qweight)[0:PLANES].reshape(PLANES, L // P, P, 2, WORDS).transpose(1, 3, 2, 0, 4)
                      .reshape(DQ_STEPS, P, PLANES, WORDS)),
        "lut4_steps": lay(np.repeat(np.asarray(L0_ffn_lut4).reshape(L // P, P, LUT), 2, axis=0)),
        "bias_rows": lay(np.broadcast_to(np.asarray(L0_ffn_bias)[None, :], (P, L))),
        **shape_constants(),
    }
    nc = bacc.Bacc("TRN2", target_bir_lowering=False, num_devices=1)
    aps = {n: nc.dram_tensor("in_" + n, v.shape, mybir.dt.from_np(v.dtype), kind="ExternalInput").ap() for n, v in arrays.items()}
    out = nc.dram_tensor("out_h", (TILES, P, L), F32, kind="ExternalOutput").ap()
    build(nc, aps, out)
    r = run_bass_kernel_spmd(nc, [{"in_" + n: v for n, v in arrays.items()}], core_ids=[0])
    return r.results[0]["out_h"].reshape(IMAGES, T, L)
```

```python
from contextlib import ExitStack

import numpy as np

import concourse.bass as bass
import concourse.mybir as mybir

F32, F16, I32, U16 = mybir.dt.float32, mybir.dt.float16, mybir.dt.int32, mybir.dt.uint16
ALU, ACT, AX = mybir.AluOpType, mybir.ActivationFunctionType, mybir.AxisListType

P = 128
IMAGES, T, N = 32, 64, 64
L = 1024
TOKENS = IMAGES * T
TILES = TOKENS // P
IMGS = P // T
HEADS, HD = 32, 32
KT = L // P
HALF = 512
L1, L2, L3, L4 = 4, 256, 16, 16
HC = 4
STAGES = 4
CHUNKS = T // HC
PIECES = 4 * KT
XS, WS = 16.0, 64.0
PS = 256.0
EPS = 1e-5
MAGIC = 12582912.0
TWO_PI = 6.2831854820251465
UNDER_TWO_PI = 6.283185005187988
COLS = {"x1": (0, 16), "x2": (16, 16), "y1": (32, 16), "y2": (48, 16), "p1": (64, 4), "p2": (68, 4), "ar": (72, 1), "ai": (73, 1)}
J = 74
XC, YC, PC, AC = slice(0, 16), slice(16, 32), slice(32, 36), slice(36, 37)
JM = 37
CH = 8
NCH = HEADS // CH
VW = HD + 1
LUT = 16
PLANES = 4
WORDS = 16
DQ_STEPS = 2 * L // P
TERMS = LUT - 1


def shape_constants():
    p = np.arange(P)
    t = p % T
    cos, sin = np.cos(t.astype(np.float64)), np.sin(t.astype(np.float64))
    q_scale = XS / (XS * WS)
    rot = np.stack([cos * q_scale, sin * q_scale, -sin * q_scale], 1).astype(np.float32)
    mask = np.where(np.arange(T)[None, :] <= t[:, None], 0.0, -1e30).astype(np.float32)
    m = np.concatenate([16.0 * np.arange(L3), np.arange(L4), 256.0 * np.arange(L1), [1.0]])
    mults = np.broadcast_to(m, (P, JM)).astype(np.float32)
    shifts = np.zeros((P, PLANES * 4 + PLANES * 4 + 8), np.int32)
    shifts[:, 0:16] = np.tile(np.arange(4), PLANES)
    shifts[:, 16:32] = np.repeat(np.arange(PLANES), 4)
    shifts[:, 32:40] = 4 * np.arange(8)
    return {"c_ident": np.eye(P, dtype=np.float32), "c_rot": rot, "c_mask": mask,
            "c_mults": np.ascontiguousarray(mults), "c_shifts": shifts}


def build(nc, a, out):
    ctx = ExitStack()
    with ctx:
        def sb(name, shape, dt):
            return ctx.enter_context(nc.sbuf_tensor("s_" + name, shape, dt))

        def sem(name):
            return ctx.enter_context(nc.semaphore(name))

        h0_dram = nc.dram_tensor("h0_scratch", (L1, IMAGES, T, L2), F32, kind="Internal").ap()
        h1_dram = nc.dram_tensor("h1_scratch", (TILES, P, L), F32, kind="Internal").ap()
        wf_dram = nc.dram_tensor("wf_scratch", (P, 4 * 2, DQ_STEPS, P), F16, kind="Internal").ap()
        h0_rows = h0_dram.rearrange("a c h l -> a (c h) l").rearrange("a (n p) l -> n p a l", p=P)

        weights = sb("weights", [P, PIECES, 2, L], F16)
        ident = sb("ident", [P, P], F32)
        rot_c = sb("rot_c", [P, 3], F32)
        mask = sb("mask", [P, T], F32)
        shifts = sb("shifts", [P, 40], I32)
        minus_half = sb("minus_half", [P, 1], F32)
        eps = sb("eps", [P, 1], F32)
        half_pi = sb("half_pi", [P, 2], F32)
        carrier = sb("carrier", [1, 2], F32)

        WORK = 20150
        work = sb("work", [P, WORK], F32)

        def carver():
            at = [0]

            def carve(dt, *shape):
                n = int(np.prod(shape))
                words = n if dt in (F32, I32) else (n + 1) // 2
                v = work[:, at[0]:at[0] + words]
                at[0] += words
                assert at[0] <= WORK, at[0]
                if dt != F32:
                    v = v.bitcast(dt)[:, 0:n]
                names = "abcd"[:len(shape)]
                if len(shape) > 1:
                    v = v.rearrange(f"p ({' '.join(names)}) -> p {' '.join(names)}", **dict(zip(names, shape)))
                return v
            return carve

        A = carver()
        w_stage = A(F32, STAGES, L)
        table = A(F32, T, J)
        abslog, phase = A(F32, T), A(F32, T)
        gr, gi, g_t1, g_t2, g_t3 = (A(F32, T) for _ in range(5))
        gp1, gp2, gp_t = (A(F32, T, L1) for _ in range(3))
        mults_s = A(F32, JM)
        q1_pow, q2_pow = A(F32, 2, HC, L2), A(F32, 2, HC, L2)
        w_pow, w_tmp = A(F32, 2, HC, L1 * IMAGES), A(F32, 2, HC, L1 * IMAGES)
        h0_stage = A(F32, 2, HC, L2)
        c_in = A(F32, STAGES, HC, 2, IMAGES)
        A2 = carver()
        A2(F32, STAGES * L + T * J + 7 * T + 3 * T * L1 + JM)
        turns, turns_abs, powers = (A2(F32, T, JM) for _ in range(3))
        B = carver()
        scores = B(F32, 2, CH, T)
        o_n = B(F32, L)
        o_t = B(F16, 2, KT, P)
        p_t = B(F16, 2, CH, P)
        h_in = B(F32, L)
        x_t = B(F16, 2, KT, P)
        q_t, k_t = B(F16, 2, KT, P), B(F16, 2, KT, P)
        q3, k3 = B(F16, HEADS, P), B(F16, HEADS, P)
        rot = B(F32, L)
        h_res = rot
        v_hi, v_lo = B(F16, HEADS, VW), B(F16, HEADS, VW)
        probs = B(F32, 2, CH, P)
        dq_words = B(I32, PLANES, WORDS)
        dq_lut = B(F32, LUT)
        dq_w = B(F32, HALF)
        dq_term = B(F32, 2, HALF)
        dq_idx = B(U16, HALF)
        dq_mask = B(U16, 4, HALF)
        dq_planes = dq_mask[:, 3].bitcast(I32).rearrange("p (w a) -> p w a", w=WORDS)
        dq_t = B(F16, 4, 2, P)
        stats, statc = B(F32, 12), B(F32, 12)
        mv, mvc = B(F32, 2), B(F32, 2)
        rstd, rstdc = B(F32, 2), B(F32, 2)
        mx = B(F32, 2, CH)
        inv = B(F32, CH)
        C = carver()
        C(F32, 3 * L)
        bias = C(F32, L)
        SLOTS = 4
        hc = C(F32, SLOTS, L)
        xc_t = C(F16, 2, 2, KT, P)
        xn = C(F32, 2, L)
        wf = weights[:, 0:KT, :, :].rearrange("p k s o -> p (k s o)").rearrange("p (k s t o) -> p k s t o", k=4, s=2, t=DQ_STEPS)

        banks = [ctx.enter_context(nc.psum_tensor(f"bank{i}", [P, HALF], F32)) for i in range(8)]
        G, M = banks[0:3], banks[3:7]
        out_bank = banks[7]

        S = {n: sem(n) for n in (
            "const_loaded ab_loaded c_loaded_0 c_loaded_1 c_loaded_2 c_loaded_3 w_loaded_0 w_loaded_1 w_loaded_2 "
            "w_loaded_3 table_step turns_ready table_sin logs_ready powers_ready table_ready x_ready gp_ready "
            "q1_ready q2_ready w_mult wt_mult w_ready mixed h0_copied h0_stored_0 h0_stored_1 w_hi w_lo h_loaded "
            "dq_masked dq_termed dq_sum ln_step var_ready rstd_ready xn_ready xt_pe xt_hi xt_lo q_pe q_scaled "
            "q_rotated qt_pe qt_hi qt_lo q_stacked k_pe k_scaled k_rotated kt_pe kt_hi kt_lo k_stacked v_pe "
            "v_hi_ready v_lo_ready s_pe s_masked s_max s_sub s_exp pt_pe pt_hi pt_lo av_pe av_inv o_ready ot_pe ot_hi "
            "ot_lo wo_pe h1_ready res_loaded h1_stored zeros_ready dq_loaded lut_loaded dq_step dqt_pe dqt_hi dqt_lo "
            "dq_stored wf_loaded wf_last_loaded var_eps_ready cvar_eps_ready carrier_ready bias_loaded hc_loaded_0 "
            "hc_loaded_1 hc_loaded_2 hc_loaded_3 cln_step cvar_ready crstd_ready cxn_ready cb_ready cxt_pe cxt_hi "
            "cxt_lo f_pe f_out out_stored_0 out_stored_1 out_stored_2 out_stored_3").split()}

        class Step:

            def __init__(self, engine, s, per_turn=0, turn=0):
                self.engine, self.s, self.per, self.turn, self.n = engine, s, per_turn, turn, 0

            def link(self, ins):
                self.n += 1
                ins.then_inc(self.s, 1)
                self.engine.wait_ge(self.s, self.turn * self.per + self.n)

        block = ctx.enter_context(nc.Block())

        def wait_ahead(s, count):
            nc.vector.wait_ge(s, count)
            nc.vector.tensor_copy(carrier[0:1, 1:2], carrier[0:1, 0:1])

        def col(name):
            s, n = COLS[name]
            return slice(s, s + n)

        @block.sync
        def _(sp):
            for dst, name in ((abslog, "abslog_t"), (phase, "phase_t"), (mults_s, "c_mults")):
                sp.dma_start(dst, a[name]).then_inc(S["ab_loaded"], 16)
            for dst, name in ((ident[:], "c_ident"), (rot_c[:], "c_rot"), (mask[:], "c_mask"), (shifts[:], "c_shifts")):
                sp.dma_start(dst, a[name]).then_inc(S["const_loaded"], 16)

            def load_piece(m, slot, first=False):
                if not first:
                    sp.wait_ge(S["w_lo"], m - STAGES + 1)
                sp.dma_start(w_stage[:, slot], a["w_t"][m]).then_inc(S[f"w_loaded_{slot}"], 16)

            def load_pieces(m0, m1):
                with sp.Fori(m0 // STAGES, m1 // STAGES) as g:
                    for slot in range(STAGES):
                        load_piece(STAGES * g + slot, slot)

            def load_c_chunk(n, slot, first=False):
                if not first:
                    sp.wait_ge(S["w_ready"], n - STAGES + 1)
                sp.dma_start(c_in[:, slot], a["c_t"][n]).then_inc(S[f"c_loaded_{slot}"], 16)

            def mixer_store(n, par):
                sp.wait_ge(S["h0_copied"], 2 * n + 2)
                sp.dma_start(h0_dram[:, :, bass.ds(n * HC, HC)].rearrange("a c h l -> (a c) h l"),
                             h0_stage[:, par]).then_inc(S[f"h0_stored_{par}"], 16)

            for n in range(STAGES):
                load_c_chunk(n, n, True)
            for m in range(STAGES):
                load_piece(m, m, True)

            def four_chunks(g, last=False):
                for k in range(STAGES):
                    n = STAGES * g + k
                    if not last:
                        load_c_chunk(n + STAGES, k)
                    load_piece(n + STAGES, k)
                    mixer_store(n, k % 2)
            with sp.Fori(0, CHUNKS // STAGES - 1) as g:
                four_chunks(g)
            four_chunks(CHUNKS // STAGES - 1, last=True)
            for par in range(2):
                sp.wait_ge(S[f"h0_stored_{par}"], 16 * CHUNKS // 2)

            def load_h(t):
                sp.dma_start(h_in.rearrange("p (a l) -> p a l", a=L1), h0_rows[t]).then_inc(S["h_loaded"], 16)

            def stack(src, dst, order, t, stacked, s_hi, s_lo):
                sp.wait_ge(S["s_pe"], 2 * NCH * t)
                sp.wait_ge(s_hi, 2 * t + 2)
                sp.wait_ge(s_lo, 2 * t + 2)
                for j in range(4):
                    for r, part in enumerate(order):
                        d = dst[32 * r:32 * r + 32].rearrange("p (k j) t -> p k j t", j=4)[:, :, j]
                        sp.dma_start(d, src[32 * j:32 * j + 32, part]).then_inc(stacked, 16)

            def turn(t, more, more_ln):
                if more_ln:
                    sp.wait_ge(S["xt_pe"], 2 * t + 4)
                    load_h(t + 2)
                if not (isinstance(t, int) and t == 0):
                    sp.wait_ge(S["dq_sum"], TERMS * t)
                sp.dma_start(dq_words, a["qwords"][t]).then_inc(S["dq_loaded"], 16)
                sp.dma_start(dq_lut, a["lut4_steps"][t]).then_inc(S["lut_loaded"], 16)
                if more:
                    stack(q_t, q3, (0, 1, 0), t + 1, S["q_stacked"], S["qt_hi"], S["qt_lo"])
                    stack(k_t, k3, (0, 0, 1), t + 1, S["k_stacked"], S["kt_hi"], S["kt_lo"])
                    sp.wait_ge(S["kt_pe"], 2 * t + 4)
                else:
                    sp.wait_ge(S["h1_stored"], 16 * t)
                sp.dma_start(h_res.rearrange("p (a l) -> p a l", a=L1), h0_rows[t]).then_inc(S["res_loaded"], 16)
                if not more:
                    prefetch_c()
                sp.wait_ge(S["dqt_lo"], t + 1)
                if more:
                    sp.dma_start(wf_dram[:, :, t, :], dq_t.rearrange("p k s o -> p (k s) o")).then_inc(S["dq_stored"], 16)
                else:
                    sp.dma_start(wf[:, :, :, t, :].rearrange("p k s o -> p (k s) o"),
                                 dq_t.rearrange("p k s o -> p (k s) o")).then_inc(S["wf_last_loaded"], 16)
                sp.wait_ge(S["h1_ready"], 2 * t + 2)
                sp.dma_start(h1_dram[t], h_res).then_inc(S["h1_stored"], 16)

            def load_c(t, slot):
                sp.dma_start(hc[:, slot], h1_dram[t]).then_inc(S[f"hc_loaded_{slot}"], 16)

            def prefetch_c():
                sp.wait_ge(S["v_pe"], 2 * TILES)
                sp.wait_ge(S["q_stacked"], 16 * 12 * TILES)
                sp.wait_ge(S["k_stacked"], 16 * 12 * TILES)
                for slot in range(SLOTS):
                    load_c(slot, slot)
                sp.wait_ge(S["dq_stored"], 16 * (DQ_STEPS - 1))
                for k in range(4):
                    sp.dma_start(wf[:, k, :, 0:DQ_STEPS - 1], wf_dram[:, 2 * k:2 * k + 2, 0:DQ_STEPS - 1]).then_inc(S["wf_loaded"], 16)
                sp.wait_ge(S["av_pe"], NCH * TILES)
                sp.dma_start(bias, a["bias_rows"]).then_inc(S["bias_loaded"], 16)

            load_h(0)
            sp.wait_ge(S["xt_pe"], 2)
            load_h(1)
            load_pieces(CHUNKS + STAGES, 3 * KT + KT // 2)
            stack(q_t, q3, (0, 1, 0), 0, S["q_stacked"], S["qt_hi"], S["qt_lo"])
            load_pieces(3 * KT + KT // 2, PIECES)
            stack(k_t, k3, (0, 0, 1), 0, S["k_stacked"], S["kt_hi"], S["kt_lo"])
            turn(0, True, True)
            with sp.Fori(1, TILES - 2) as t:
                turn(t, True, True)
            turn(TILES - 2, True, False)
            turn(TILES - 1, False, False)

            sp.wait_ge(S["h1_stored"], 16 * TILES)

            def four(g, first=False, last=False):
                for slot in range(SLOTS):
                    t = SLOTS * g + slot
                    sp.wait_ge(S["f_out"], 2 * t + 2)
                    sp.dma_start(out[t], hc[:, slot]).then_inc(S[f"out_stored_{slot}"], 16)
                    if slot and not last:
                        sp.wait_ge(S[f"out_stored_{slot - 1}"], 16 * g + 16)
                        load_c(t + 3, slot - 1)
                    elif not slot and not first:
                        sp.wait_ge(S[f"out_stored_{SLOTS - 1}"], 16 * g)
                        load_c(t + 3, SLOTS - 1)
            four(0, first=True)
            with sp.Fori(1, TILES // SLOTS - 1) as g:
                four(g)
            four(TILES // SLOTS - 1, last=True)
            for slot in range(SLOTS):
                sp.wait_ge(S[f"out_stored_{slot}"], 16 * TILES // SLOTS)

        @block.tensor
        def _(pe):
            def mix(g, par, first=False):
                n = 2 * g + par
                for ready in ("w_ready", "q1_ready", "q2_ready"):
                    pe.wait_ge(S[ready], n + 1)
                if not first:
                    pe.wait_ge(S["h0_copied"], 2 * n - 2)
                for h in range(HC):
                    o = banks[2 * par + h // 2][:, (h % 2) * L2:(h % 2 + 1) * L2]
                    nc.tensor.matmul(o, w_pow[:, par, h], q1_pow[:, par, h], start=True, stop=False)
                    last = nc.tensor.matmul(o, w_pow[:, par, h], q2_pow[:, par, h], start=False, stop=True)
                    if h % 2:
                        last.then_inc(S["mixed"], 1)
            mix(0, 0, True)
            mix(0, 1, True)
            with pe.Fori(1, CHUNKS // 2) as g:
                mix(g, 0)
                mix(g, 1)

            def transpose8(src, b0, b1, done):
                for k in range(KT):
                    last = nc.tensor.transpose((b0 if k < 4 else b1)[:, (k % 4) * P:(k % 4 + 1) * P],
                                               src[:, k * P:(k + 1) * P], ident[:])
                    if k % 4 == 3:
                        last.then_inc(done, 1)

            def product(bank, x, w, half, done, part=(0, KT)):
                for k in range(*part):
                    for n, (xp, wp) in enumerate(((0, 0), (0, 1), (1, 0))):
                        last = nc.tensor.matmul(bank[:, :], x[:, xp, k], w(k, wp, half), start=(k == 0 and n == 0),
                                                stop=(k == KT - 1 and n == 2))
                if part[1] == KT:
                    last.then_inc(done, 1)

            def w_of(mat):
                return lambda k, part, half: weights[:, mat * KT + k, part, half * HALF:(half + 1) * HALF]

            FRONT, BACK = (0, KT // 2), (KT // 2, KT)
            Q, K, V, O = (w_of(m) for m in range(4))

            def x_transposes(t):
                pe.wait_ge(S["xn_ready"], t + 1)
                pe.wait_ge(S["kt_lo"], 2 * t)
                transpose8(h_in, M[2], M[3], S["xt_pe"])

            def weight_transposes(t):
                pe.wait_ge(S["dq_sum"], TERMS * (t + 1))
                for k in range(4):
                    last = nc.tensor.transpose(out_bank[:, k * P:(k + 1) * P], dq_w[:, k * P:(k + 1) * P], ident[:])
                last.then_inc(S["dqt_pe"], 1)

            def body(t, att, qkv, ln):
                u = t + 1
                if qkv:
                    pe.wait_ge(S["xt_lo"], 2 * u + 2)
                    if att and not (isinstance(t, int) and t == 0):
                        pe.wait_ge(S["h1_ready"], 2 * t - 1)
                    product(G[0], x_t, Q, 0, S["q_pe"], FRONT)
                if att:
                    pe.wait_ge(S["q_stacked"], 16 * 12 * (t + 1))
                    pe.wait_ge(S["k_stacked"], 16 * 12 * (t + 1))

                def score_chunk(c):
                    for b in range(2):
                        if c:
                            pe.wait_ge(S["s_masked"], 16 * t + 4 * c - 2 + 2 * b)
                        for h in range(4):
                            head = c * CH + b * 4 + h
                            last = nc.tensor.matmul(M[b][:, h * P:(h + 1) * P], q3[0:96, head], k3[0:96, head],
                                                    start=True, stop=True)
                        last.then_inc(S["s_pe"], 1)

                def prob_transposes(c):
                    pe.wait_ge(S["s_exp"], 8 * t + 2 * c + 2)
                    for b in range(2):
                        if c:
                            pe.wait_ge(S["pt_lo"], 8 * t + 2 * c - 1 + b)
                        for h in range(4):
                            last = nc.tensor.transpose(M[2 + b][:, h * P:(h + 1) * P], probs[:, c % 2, b * 4 + h], ident[:])
                        last.then_inc(S["pt_pe"], 1)

                def values_chunk(c):
                    pe.wait_ge(S["pt_lo"], 8 * t + 2 * c + 2)
                    if c == 0:
                        pe.wait_ge(S["v_lo_ready"], 2 * t + 2)
                    if c >= 1:
                        pe.wait_ge(S["o_ready"], 4 * t + c)
                    for h in range(CH):
                        head = c * CH + h
                        o = out_bank[:, h * VW:(h + 1) * VW]
                        nc.tensor.matmul(o, p_t[:, 0, h], v_hi[:, head], start=True, stop=False)
                        nc.tensor.matmul(o, p_t[:, 0, h], v_lo[:, head], start=False, stop=False)
                        last = nc.tensor.matmul(o, p_t[:, 1, h], v_hi[:, head], start=False, stop=True)
                    last.then_inc(S["av_pe"], 1)

                if att:
                    if not (isinstance(t, int) and t == 0):
                        pe.wait_ge(S["ot_lo"], 2 * t)
                    score_chunk(0)
                if qkv:
                    product(G[0], x_t, Q, 0, S["q_pe"], BACK)
                if att:
                    score_chunk(1)
                if qkv:
                    if att:
                        pe.wait_ge(S["h1_ready"], 2 * t)
                    product(G[1], x_t, Q, 1, S["q_pe"], FRONT)
                if att and not qkv:
                    score_chunk(2)
                    prob_transposes(0)
                    score_chunk(3)
                elif att:
                    prob_transposes(0)
                    score_chunk(2)
                if qkv:
                    product(G[1], x_t, Q, 1, S["q_pe"], BACK)
                    product(G[2], x_t, K, 0, S["k_pe"], FRONT)
                if att:
                    pe.wait_ge(S["dqt_lo"], t)
                    values_chunk(0)
                    prob_transposes(1)
                    if qkv:
                        score_chunk(3)
                if qkv:
                    product(G[2], x_t, K, 0, S["k_pe"], BACK)
                    pe.wait_ge(S["q_rotated"], 4 * u + 4)
                    if att:
                        pe.wait_ge(S["s_masked"], 16 * t + 16)
                    transpose8(rot, M[0], M[1], S["qt_pe"])
                    product(G[0], x_t, K, 1, S["k_pe"], FRONT)
                if att:
                    values_chunk(1)
                    prob_transposes(2)
                if qkv:
                    product(G[0], x_t, K, 1, S["k_pe"], BACK)
                    if not att:
                        pe.wait_ge(S["w_lo"], 3 * KT)
                    product(G[1], x_t, V, 0, S["v_pe"], FRONT)
                if att:
                    values_chunk(2)
                    prob_transposes(3)
                if qkv:
                    product(G[1], x_t, V, 0, S["v_pe"], BACK)
                if att:
                    values_chunk(3)
                if qkv:
                    pe.wait_ge(S["k_rotated"], 4 * u + 4)
                    if att:
                        pe.wait_ge(S["pt_lo"], 8 * t + 8)
                    transpose8(rot, M[2], M[3], S["kt_pe"])
                    product(G[2], x_t, V, 1, S["v_pe"], FRONT)
                if att and not qkv:
                    pe.wait_ge(S["cxn_ready"], 1)
                    pe.wait_ge(S["pt_lo"], 8 * t + 8)
                    transpose8(xn[:, 0], M[2], M[3], S["cxt_pe"])
                if att:
                    pe.wait_ge(S["o_ready"], 4 * t + 4)
                    if qkv:
                        pe.wait_ge(S["qt_lo"], 2 * u + 2)
                    transpose8(o_n, M[0], M[1], S["ot_pe"])
                if qkv:
                    product(G[2], x_t, V, 1, S["v_pe"], BACK)
                if ln:
                    x_transposes(t + 2)
                if att:
                    if isinstance(t, int) and t == 0:
                        pe.wait_ge(S["w_lo"], PIECES)
                    pe.wait_ge(S["ot_lo"], 2 * t + 2)
                    if qkv:
                        pe.wait_ge(S["v_lo_ready"], 2 * u + 1)
                    product(G[0], o_t, O, 0, S["wo_pe"])
                    if qkv:
                        weight_transposes(t)
                    product(G[1], o_t, O, 1, S["wo_pe"])
                    if not qkv:
                        weight_transposes(t)

            pe.wait_ge(S["xn_ready"], 1)
            pe.wait_ge(S["h0_copied"], 2 * CHUNKS)
            transpose8(h_in, M[2], M[3], S["xt_pe"])
            pe.wait_ge(S["xt_lo"], 2)
            pe.wait_ge(S["w_lo"], 2 * KT)
            body(-1, False, True, False)
            x_transposes(1)
            body(0, True, True, True)
            with pe.Fori(1, TILES - 2) as t:
                body(t, True, True, True)
            body(TILES - 2, True, True, False)
            body(TILES - 1, True, False, False)

            def wf_of(k, part, half):
                return wf[:, k % 4, part, :, :].rearrange("p (o h) c -> p o h c", h=2)[:, half * 4:half * 4 + 4, k // 4]

            F_BANKS = ((G[2], M[2]), (G[0], G[1]))

            def c_transposes(t, par):
                pe.wait_ge(S["cxn_ready"], t + 1)
                pe.wait_ge(S["cxt_lo"], 2 * t)
                transpose8(xn[:, par], M[0], M[1], S["cxt_pe"])

            def pair(g, first=False, last=False):
                for par in range(2):
                    t = 2 * g + par
                    pe.wait_ge(S["cxt_lo"], 2 * t + 2)
                    if not first:
                        pe.wait_ge(S["f_out"], 2 * t - 2)
                    elif par:
                        pe.wait_ge(S["h1_ready"], 2 * TILES)
                    product(F_BANKS[par][0], xc_t[:, par], wf_of, 0, S["f_pe"])
                    if not last or par == 0:
                        c_transposes(t + 1, 1 - par)
                    if first and par == 0:
                        pe.wait_ge(S["wf_last_loaded"], 16)
                    product(F_BANKS[par][1], xc_t[:, par], wf_of, 1, S["f_pe"])
            pe.wait_ge(S["wf_loaded"], 16 * 4)
            pair(0, first=True)
            with pe.Fori(1, TILES // 2 - 1) as g:
                pair(g)
            pair(TILES // 2 - 1, last=True)

        @block.scalar
        def _(act):
            act.wait_ge(S["logs_ready"], 1)
            nc.scalar.activation(powers, powers, ACT.Exp).then_inc(S["powers_ready"], 1)

            re, im, both = slice(0, N), slice(N, P), slice(0, P)

            def sine(name, rows, m, sign):
                nc.scalar.activation(table[rows, :, col(name)], turns[rows, :, m], ACT.Sin,
                                     scale=sign * UNDER_TWO_PI).then_inc(S["table_sin"], 1)

            def cosine(name, rows, m, sign):
                bias_at = half_pi[rows, 0:1] if sign > 0 else half_pi[rows, 1:2]
                nc.scalar.activation(table[rows, :, col(name)], turns_abs[rows, :, m], ACT.Sin, bias=bias_at,
                                     scale=-sign * UNDER_TWO_PI).then_inc(S["table_sin"], 1)

            act.wait_ge(S["turns_ready"], 1)
            sine("ai", both, AC, 1.0)
            sine("p1", im, PC, -1.0)
            sine("p2", re, PC, -1.0)
            sine("x2", re, XC, -1.0)
            sine("x2", im, XC, 1.0)
            act.wait_ge(S["turns_ready"], 2)
            cosine("ar", both, AC, 1.0)
            cosine("p1", re, PC, 1.0)
            cosine("p2", im, PC, -1.0)
            cosine("x1", both, XC, 1.0)
            cosine("y1", re, YC, 1.0)
            sine("y1", im, YC, 1.0)
            sine("y2", re, YC, 1.0)
            cosine("y2", im, YC, 1.0)

            def piece_hi(g, slot):
                act.wait_ge(S[f"w_loaded_{slot}"], 16 * (g + 1))
                nc.scalar.activation(weights[:, STAGES * g + slot, 0], w_stage[:, slot], ACT.Copy, scale=WS).then_inc(S["w_hi"], 1)

            def pieces_hi(m0, m1):
                for g in range(m0 // STAGES, m1 // STAGES):
                    for slot in range(STAGES):
                        piece_hi(g, slot)

            def four_chunks(g, first=False):
                for k in range(STAGES):
                    n, par = STAGES * g + k, k % 2
                    if k < STAGES - 1:
                        piece_hi(g, k + 1)
                    else:
                        piece_hi(g + 1, 0)
                    for b in range(2):
                        act.wait_ge(S["mixed"], 2 * n + b + 1)
                        if first and k < 2:
                            if b == 0:
                                act.wait_ge(S["table_ready"], 3)
                                act.wait_ge(S["x_ready"], 1)
                        else:
                            act.wait_ge(S[f"h0_stored_{par}"], 16 * (2 * g + k // 2))
                        nc.scalar.activation(h0_stage[:, par, 2 * b:2 * b + 2].rearrange("p h l -> p (h l)"),
                                             banks[2 * par + b][:, :], ACT.Copy).then_inc(S["h0_copied"], 1)
            piece_hi(0, 0)
            four_chunks(0, True)
            with act.Fori(1, CHUNKS // STAGES) as g:
                four_chunks(g)

            def hi8(dst, b0, b1, ready, done, count, scale):
                for b, bank in enumerate((b0, b1)):
                    act.wait_ge(ready, count + b + 1)
                    nc.scalar.activation(dst[:, 0, 4 * b:4 * b + 4].rearrange("p k t -> p (k t)"), bank[:, :], ACT.Copy,
                                         scale=scale).then_inc(done, 1)

            def scale_half(u, half, bank, ready, done):
                act.wait_ge(ready, 2 * u + half + 1)
                nc.scalar.activation(rot[:, half * HALF:(half + 1) * HALF], bank[:, :], ACT.Copy, scale=rot_c[:, 0:1]).then_inc(done, 1)

            def values_half(u, half, bank):
                act.wait_ge(S["v_pe"], 2 * u + half + 1)
                act.wait_ge(S["av_pe"], NCH * u)
                nc.scalar.activation(v_hi[:, 16 * half:16 * half + 16, 0:HD], bank[:, :].rearrange("p (h d) -> p h d", d=HD),
                                     ACT.Copy, scale=XS / (XS * WS)).then_inc(S["v_hi_ready"], 1)

            def body(t, att, qkv, ln):
                u = t + 1

                def exps(c):
                    act.wait_ge(S["s_sub"], 4 * t + c + 1)
                    if c >= 2:
                        act.wait_ge(S["pt_pe"], 8 * t + 2 * c - 2)
                    else:
                        act.wait_ge(S["pt_pe"], 8 * t)
                    for i in range(IMGS):
                        r = slice(i * T, i * T + T)
                        nc.scalar.activation(probs[r, c % 2, :, i * T:i * T + T], scores[r, c % 2], ACT.Exp,
                                             scale=HD ** -0.5 / (XS * XS)).then_inc(S["s_exp"], 1)

                def p_hi(c):
                    for b in range(2):
                        act.wait_ge(S["pt_pe"], 8 * t + 2 * c + b + 1)
                        if b == 0:
                            act.wait_ge(S["av_pe"], 4 * t + c)
                        nc.scalar.activation(p_t[:, 0, 4 * b:4 * b + 4].rearrange("p k t -> p (k t)"), M[2 + b][:, :],
                                             ACT.Copy, scale=PS).then_inc(S["pt_hi"], 1)

                def dq_terms(v0, v1):
                    if v0 == 0:
                        act.wait_ge(S["lut_loaded"], 16 * t + 16)
                    for v in range(v0, v1):
                        act.wait_ge(S["dq_masked"], LUT * t + v + 1)
                        if v and not (isinstance(t, int) and TERMS * t + v <= 2):
                            act.wait_ge(S["dq_sum"], TERMS * t + max(v - 2, 0))
                        nc.scalar.activation(dq_term[:, v % 2] if v else dq_w, dq_mask[:, v % 4], ACT.Copy,
                                             scale=dq_lut[:, v:v + 1]).then_inc(S["dq_termed"], 1)

                def dq_hi():
                    act.wait_ge(S["dqt_pe"], t + 1)
                    act.wait_ge(S["dq_stored"], 16 * t)
                    nc.scalar.activation(dq_t[:, :, 0], out_bank[:, :].rearrange("p (k o) -> p k o", k=4), ACT.Copy,
                                         scale=WS).then_inc(S["dqt_hi"], 1)

                if not qkv:
                    exps(0)
                    p_hi(0)
                    exps(1)
                    dq_terms(0, 2)
                    exps(2)
                    p_hi(1)
                    dq_terms(2, 4)
                    exps(3)
                    p_hi(2)
                    dq_terms(4, 6)
                    p_hi(3)
                    hi8(xc_t[:, 0], M[2], M[3], S["cxt_pe"], S["cxt_hi"], 0, XS)
                    dq_terms(6, 8)
                    act.wait_ge(S["wo_pe"], 2 * t)
                    hi8(o_t, M[0], M[1], S["ot_pe"], S["ot_hi"], 2 * t, 1.0)
                    dq_hi()
                    return

                if att:
                    exps(0)
                if qkv:
                    act.wait_ge(S["kt_pe"], 2 * u)
                    if att:
                        act.wait_ge(S["h1_stored"], 16 * t)
                    scale_half(u, 0, G[0], S["q_pe"], S["q_scaled"])
                if att:
                    p_hi(0)
                    exps(1)
                    dq_terms(0, 2)
                if qkv:
                    scale_half(u, 1, G[1], S["q_pe"], S["q_scaled"])
                if att:
                    p_hi(1)
                    dq_terms(2, 4)
                    exps(2)
                    exps(3)
                    dq_terms(4, 6)
                if qkv:
                    act.wait_ge(S["q_stacked"], 16 * 12 * u)
                    hi8(q_t, M[0], M[1], S["qt_pe"], S["qt_hi"], 2 * u, 1.0)
                    if not att:
                        pieces_hi(3 * KT, 3 * KT + KT // 2)
                    scale_half(u, 0, G[2], S["k_pe"], S["k_scaled"])
                if att:
                    dq_terms(6, 8)
                    p_hi(2)
                if qkv:
                    scale_half(u, 1, G[0], S["k_pe"], S["k_scaled"])
                if att:
                    p_hi(3)
                    dq_terms(8, 12)
                if qkv:
                    act.wait_ge(S["k_stacked"], 16 * 12 * u)
                    hi8(k_t, M[2], M[3], S["kt_pe"], S["kt_hi"], 2 * u, 1.0)
                    if not att:
                        act.wait_ge(S["zeros_ready"], 1)
                    values_half(u, 0, G[1])
                if att:
                    dq_terms(12, 14)
                    act.wait_ge(S["wo_pe"], 2 * t)
                    hi8(o_t, M[0], M[1], S["ot_pe"], S["ot_hi"], 2 * t, 1.0)
                    dq_terms(14, 16)
                if qkv:
                    values_half(u, 1, G[2])
                if ln:
                    hi8(x_t, M[2], M[3], S["xt_pe"], S["xt_hi"], 2 * t + 4, XS)
                if att:
                    dq_hi()

            act.wait_ge(S["const_loaded"], 64)
            hi8(x_t, M[2], M[3], S["xt_pe"], S["xt_hi"], 0, XS)
            for m in range(2 * KT + 1, 3 * KT):
                piece_hi(m // STAGES, m % STAGES)
            body(-1, False, True, False)
            hi8(x_t, M[2], M[3], S["xt_pe"], S["xt_hi"], 2, XS)
            pieces_hi(3 * KT + KT // 2, PIECES)
            body(0, True, True, True)
            with act.Fori(1, TILES - 2) as t:
                body(t, True, True, True)
            body(TILES - 2, True, True, False)
            body(TILES - 1, True, False, False)

            def c_turn(t, par):
                act.wait_ge(S["f_pe"], 2 * t - 2) if not (isinstance(t, int) and t < 2) else None
                hi8(xc_t[:, par], M[0], M[1], S["cxt_pe"], S["cxt_hi"], 2 * t, XS)
            c_turn(1, 1)
            with act.Fori(1, TILES // 2) as g:
                for par in range(2):
                    c_turn(2 * g + par, par)

        @block.vector
        def _(dve):
            V = nc.vector
            st = Step(dve, S["table_step"])
            V.memset(minus_half[:], -0.5)
            V.memset(eps[:], EPS)
            V.memset(half_pi[:, 0:1], TWO_PI / 4)
            V.memset(half_pi[:, 1:2], -TWO_PI / 4)
            V.memset(carrier[:], 0.0).then_inc(S["carrier_ready"], 1)
            dve.wait_ge(S["carrier_ready"], 1)
            dve.wait_ge(S["ab_loaded"], 48)
            ph_k, u_turn = g_t1, g_t2
            st.link(V.tensor_scalar(ph_k, phase, 1.0 / TWO_PI, MAGIC, ALU.mult, ALU.add))
            st.link(V.tensor_scalar(ph_k, ph_k, MAGIC, None, ALU.subtract))
            st.link(V.scalar_tensor_tensor(phase, ph_k, -TWO_PI, phase, ALU.mult, ALU.add))
            st.link(V.tensor_scalar(u_turn, phase, 1.0 / TWO_PI, None, ALU.mult))
            full = [P, T, JM]
            st.link(V.tensor_tensor(turns, u_turn.unsqueeze(2).broadcast_to(full), mults_s.unsqueeze(1).broadcast_to(full), ALU.mult))
            st.link(V.tensor_scalar(turns_abs, turns, MAGIC, MAGIC, ALU.add, ALU.subtract))
            V.tensor_tensor(turns, turns, turns_abs, ALU.subtract).then_inc(S["turns_ready"], 1)
            dve.wait_ge(S["turns_ready"], 1)
            V.scalar_tensor_tensor(turns_abs, turns, -1.0, turns, ALU.mult, ALU.max).then_inc(S["turns_ready"], 1)
            st.link(V.tensor_tensor(g_t1, abslog, abslog, ALU.mult))
            st.link(V.tensor_tensor(g_t3, phase, phase, ALU.mult))
            st.link(V.tensor_tensor(g_t1, g_t1, g_t3, ALU.add))
            st.link(V.reciprocal(g_t1, g_t1))

            def times_powers(first, n, m):
                shape = [P, T, 2, n]
                v = table[:, :, first:first + 2 * n].rearrange("p t (two n) -> p t two n", two=2)
                V.tensor_tensor(v, v, powers[:, :, m].unsqueeze(2).broadcast_to(shape), ALU.mult).then_inc(S["table_ready"], 1)

            dve.wait_ge(S["powers_ready"], 1)
            dve.wait_ge(S["table_sin"], 8)
            times_powers(COLS["ar"][0], 1, AC)
            times_powers(COLS["p1"][0], L1, PC)
            ar, ai = table[:, :, col("ar")], table[:, :, col("ai")]
            a3 = lambda x: x.unsqueeze(2)
            dve.wait_ge(S["table_ready"], 2)
            st.link(V.tensor_scalar(ar, ar, 1.0, None, ALU.subtract))
            V.tensor_tensor(a3(gr), ar, a3(abslog), ALU.mult).then_inc(S["table_step"], 1)
            V.tensor_tensor(a3(g_t2), ai, a3(phase), ALU.mult).then_inc(S["table_step"], 1)
            V.tensor_tensor(a3(gi), ai, a3(abslog), ALU.mult).then_inc(S["table_step"], 1)
            st.n += 3
            st.link(V.tensor_tensor(a3(g_t3), ar, a3(phase), ALU.mult))
            V.tensor_tensor(gr, gr, g_t2, ALU.add).then_inc(S["table_step"], 1)
            st.n += 1
            st.link(V.tensor_tensor(gi, gi, g_t3, ALU.subtract))
            V.scalar_tensor_tensor(gr, gr, 2.0, g_t1, ALU.mult, ALU.mult).then_inc(S["table_step"], 1)
            st.n += 1
            st.link(V.scalar_tensor_tensor(gi, gi, 2.0, g_t1, ALU.mult, ALU.mult))
            s4 = [P, T, L1]
            p1, p2 = table[:, :, col("p1")], table[:, :, col("p2")]
            gr4, gi4 = a3(gr).broadcast_to(s4), a3(gi).broadcast_to(s4)
            st.link(V.tensor_tensor(gp1, p1, gr4, ALU.mult))
            st.link(V.tensor_tensor(gp_t, p2, gi4, ALU.mult))
            st.link(V.tensor_tensor(gp1, gp1, gp_t, ALU.add))
            st.link(V.tensor_tensor(gp2, p2, gr4, ALU.mult))
            st.link(V.tensor_tensor(gp_t, p1, gi4, ALU.mult))
            V.tensor_tensor(gp2, gp2, gp_t, ALU.subtract).then_inc(S["gp_ready"], 1)
            dve.wait_ge(S["table_sin"], 13)
            times_powers(COLS["y1"][0], L4, YC)
            dve.wait_ge(S["gp_ready"], 1)
            dve.wait_ge(S["table_ready"], 3)
            dve.wait_ge(S["x_ready"], 1)

            def piece_lo(m, slot):
                dve.wait_ge(S["w_hi"], m + 1)
                V.scalar_tensor_tensor(weights[:, m, 1], w_stage[:, slot], WS, weights[:, m, 0], ALU.mult,
                                       ALU.subtract).then_inc(S["w_lo"], 1)

            def pieces_lo(m0, m1):
                for m in range(m0, m1):
                    piece_lo(m, m % STAGES)

            def four_chunks(g, first=False):
                for k in range(STAGES):
                    n, par = STAGES * g + k, k % 2
                    hs = bass.ds(n * HC, HC)
                    sq, sw = [P, HC, L3, L4], [P, HC, L1, IMAGES]
                    if not (first and k < 2):
                        dve.wait_ge(S["mixed"], 2 * (n - 1))
                    dve.wait_ge(S[f"c_loaded_{k}"], 16 * (g + 1))
                    w4 = w_pow[:, par].rearrange("p h (a b) -> p h a b", b=IMAGES)
                    V.tensor_tensor(w4, c_in[:, k, :, 0].unsqueeze(2).broadcast_to(sw), gp1[:, hs].unsqueeze(3).broadcast_to(sw),
                                    ALU.mult).then_inc(S["w_mult"], 1)
                    V.tensor_tensor(q1_pow[:, par].rearrange("p h (a b) -> p h a b", b=L4),
                                    table[:, hs, col("x1")].unsqueeze(3).broadcast_to(sq),
                                    table[:, hs, col("y1")].unsqueeze(2).broadcast_to(sq), ALU.mult).then_inc(S["q1_ready"], 1)
                    dve.wait_ge(S["wt_mult"], n + 1)
                    dve.wait_ge(S["w_mult"], n + 1)
                    V.tensor_tensor(w_pow[:, par], w_pow[:, par], w_tmp[:, par], ALU.add).then_inc(S["w_ready"], 1)
                    piece_lo(n, k)
            four_chunks(0, True)
            with dve.Fori(1, CHUNKS // STAGES) as g:
                four_chunks(g)

            def lo8(dst, b0, b1, ready, done, count, scale):
                for b, bank in enumerate((b0, b1)):
                    dve.wait_ge(ready, count + b + 1)
                    V.scalar_tensor_tensor(dst[:, 1, 4 * b:4 * b + 4].rearrange("p k t -> p (k t)"), bank[:, :], scale,
                                           dst[:, 0, 4 * b:4 * b + 4].rearrange("p k t -> p (k t)"), ALU.mult,
                                           ALU.subtract).then_inc(done, 1)

            def norm_stats(x, stat, mean_var, t, loaded, step, var):
                dve.wait_ge(*loaded)
                V.bn_stats(stat[:, 0:6], x[:, 0:HALF]).then_inc(step, 1)
                V.bn_stats(stat[:, 6:12], x[:, HALF:L]).then_inc(step, 1)
                wait_ahead(step, 2 * t + 2)
                V.bn_aggr(mean_var, stat).then_inc(var, 1)

            def norm_stats_b(t):
                norm_stats(h_in, stats, mv, t, (S["h_loaded"], 16 * t + 16), S["ln_step"], S["var_ready"])

            def norm_b(t):
                dve.wait_ge(S["rstd_ready"], t + 1)
                V.tensor_scalar(h_in, h_in, mv[:, 0:1], rstd[:, 1:2], ALU.subtract, ALU.mult).then_inc(S["xn_ready"], 1)

            def rotate_half(u, half, bank, ready, done):
                dve.wait_ge(ready, 2 * u + half + 1)
                b = bank[:, :].rearrange("p (d two) -> p two d", two=2)
                o = rot[:, half * HALF:(half + 1) * HALF].rearrange("p (d two) -> p two d", two=2)
                V.scalar_tensor_tensor(o[:, 0], b[:, 1], rot_c[:, 2:3], o[:, 0], ALU.mult, ALU.add).then_inc(done, 1)
                V.scalar_tensor_tensor(o[:, 1], b[:, 0], rot_c[:, 1:2], o[:, 1], ALU.mult, ALU.add).then_inc(done, 1)

            def values_half(u, half, bank):
                dve.wait_ge(S["v_hi_ready"], 2 * u + half + 1)
                hs = slice(16 * half, 16 * half + 16)
                V.scalar_tensor_tensor(v_lo[:, hs, 0:HD], bank[:, :].rearrange("p (h d) -> p h d", d=HD), XS / (XS * WS),
                                       v_hi[:, hs, 0:HD], ALU.mult, ALU.subtract).then_inc(S["v_lo_ready"], 1)

            def stats_c(t, g, slot):
                norm_stats(hc[:, slot], statc, mvc, t, (S[f"hc_loaded_{slot}"], 16 * g + 16), S["cln_step"], S["cvar_ready"])

            def norm_c(t, slot, first=False):
                if not first:
                    dve.wait_ge(S["cxt_pe"], 2 * t - 2)
                dve.wait_ge(S["crstd_ready"], t + 1)
                V.tensor_scalar(xn[:, slot % 2], hc[:, slot], mvc[:, 0:1], rstdc[:, 1:2], ALU.subtract,
                                ALU.mult).then_inc(S["cxn_ready"], 1)

            def bias_c(t, slot):
                dve.wait_ge(S["cxn_ready"], t + 1)
                V.tensor_tensor(hc[:, slot], hc[:, slot], bias, ALU.add).then_inc(S["cb_ready"], 1)

            DQ = PLANES + 7

            def body(t, att, qkv, ln):
                u = t + 1
                dq = Step(dve, S["dq_step"], DQ, t)

                def masked(c):
                    for b in range(2):
                        dve.wait_ge(S["s_pe"], 8 * t + 2 * c + b + 1)
                        if b == 0:
                            dve.wait_ge(S["s_exp"], 8 * t + 2 * c - 2 if c >= 2 else 8 * t)
                        for i in range(IMGS):
                            r = slice(i * T, i * T + T)
                            src = M[b][r, :].rearrange("p (h s) -> p h s", h=4)[:, :, i * T:i * T + T]
                            V.tensor_tensor(scores[r, c % 2, 4 * b:4 * b + 4], src, mask[r, :].unsqueeze(1).broadcast_to([T, 4, T]),
                                            ALU.add).then_inc(S["s_masked"], 1)
                    dve.wait_ge(S["s_masked"], 16 * t + 4 * c + 4)
                    V.reduce_max(mx[:, c % 2], scores[:, c % 2], AX.X).then_inc(S["s_max"], 1)

                def p_lo(c):
                    for b in range(2):
                        dve.wait_ge(S["pt_hi"], 8 * t + 2 * c + b + 1)
                        V.scalar_tensor_tensor(p_t[:, 1, 4 * b:4 * b + 4].rearrange("p k t -> p (k t)"), M[2 + b][:, :], PS,
                                               p_t[:, 0, 4 * b:4 * b + 4].rearrange("p k t -> p (k t)"), ALU.mult,
                                               ALU.subtract).then_inc(S["pt_lo"], 1)

                def normalise(c):
                    dve.wait_ge(S["av_pe"], 4 * t + c + 1)
                    o = out_bank[:, 0:CH * VW].rearrange("p (h d) -> p h d", d=VW)
                    V.reciprocal(inv.unsqueeze(2), o[:, :, HD:VW]).then_inc(S["av_inv"], 1)
                    dve.wait_ge(S["av_inv"], 4 * t + c + 1)
                    if c == 0:
                        dve.wait_ge(S["ot_pe"], 2 * t)
                    V.tensor_tensor(o_n[:, c * CH * HD:(c + 1) * CH * HD].rearrange("p (h d) -> p h d", d=HD), o[:, :, 0:HD],
                                    inv.unsqueeze(2).broadcast_to([P, CH, HD]), ALU.mult).then_inc(S["o_ready"], 1)

                def dq_index():
                    dve.wait_ge(S["dq_loaded"], 16 * t + 16)
                    dve.wait_ge(S["dqt_pe"], t)
                    dve.wait_ge(S["dq_termed"], LUT * t)
                    d4 = dq_planes.rearrange("p w (a k) -> p w a k", a=PLANES)
                    s4 = [P, WORDS, 4]
                    for pl in range(PLANES):
                        V.tensor_tensor(d4[:, :, pl], dq_words[:, pl].unsqueeze(2).broadcast_to(s4),
                                        shifts[:, 4 * pl:4 * pl + 4].unsqueeze(1).broadcast_to(s4),
                                        ALU.logical_shift_right).then_inc(S["dq_step"], 1)
                    dq.n += PLANES
                    dve.wait_ge(S["dq_step"], t * DQ + dq.n)
                    dq.link(V.tensor_scalar(dq_planes, dq_planes, 0x11111111, None, ALU.bitwise_and))

                def dq_nibbles():
                    full = [P, WORDS, PLANES * 4]
                    dq.link(V.tensor_tensor(dq_planes, dq_planes, shifts[:, 16:32].unsqueeze(1).broadcast_to(full),
                                            ALU.logical_shift_left))
                    d4 = dq_planes.rearrange("p w (a k) -> p w a k", a=PLANES)
                    dq.link(V.tensor_tensor(d4[:, :, 0:2], d4[:, :, 0:2], d4[:, :, 2:4], ALU.bitwise_or))
                    dq.link(V.tensor_tensor(d4[:, :, 0], d4[:, :, 0], d4[:, :, 1], ALU.bitwise_or))
                    full = [P, WORDS, 8, 4]
                    codes = dq_w.bitcast(I32)
                    dq.link(V.tensor_tensor(codes.rearrange("p (w m k) -> p w m k", m=8, k=4),
                                            d4[:, :, 0].unsqueeze(2).broadcast_to(full),
                                            shifts[:, 32:40].unsqueeze(1).unsqueeze(3).broadcast_to(full),
                                            ALU.logical_shift_right))
                    dq.link(V.tensor_scalar(codes, codes, 15, None, ALU.bitwise_and))
                    dq.link(V.tensor_copy(dq_idx, codes))

                def dq_masks(v0, v1, wait=True):
                    if v0 and wait:
                        dve.wait_ge(S["dq_termed"], LUT * t + v0)
                    for v in range(v0, v1):
                        V.tensor_scalar(dq_mask[:, v % 4], dq_idx, float(v), None, ALU.is_equal).then_inc(S["dq_masked"], 1)

                def dq_rest(v0, v1):
                    dve.wait_ge(S["dq_sum"], TERMS * t + v0 - 1)
                    dq_masks(v0, v1, wait=False)
                    for v in range(v0, v1):
                        dve.wait_ge(S["dq_masked"], LUT * t + v + 1)
                        dve.wait_ge(S["dq_sum"], TERMS * t + v - 1)
                        V.scalar_tensor_tensor(dq_w, dq_mask[:, v % 4], dq_lut[:, v:v + 1], dq_w, ALU.mult,
                                               ALU.add).then_inc(S["dq_sum"], 1)

                def dq_lo():
                    dve.wait_ge(S["dqt_hi"], t + 1)
                    V.scalar_tensor_tensor(dq_t[:, :, 1], out_bank[:, :].rearrange("p (k o) -> p k o", k=4), WS, dq_t[:, :, 0],
                                           ALU.mult, ALU.subtract).then_inc(S["dqt_lo"], 1)

                def residual(half):
                    dve.wait_ge(S["wo_pe"], 2 * t + half + 1)
                    r = h_res[:, half * HALF:(half + 1) * HALF]
                    V.scalar_tensor_tensor(r, (G[0], G[1])[half][:, :], 1.0 / (XS * WS), r, ALU.mult, ALU.add).then_inc(S["h1_ready"], 1)

                if not qkv:
                    masked(0)
                    masked(1)
                    dq_index()
                    masked(2)
                    p_lo(0)
                    dq_nibbles()
                    dq_masks(0, 4)
                    masked(3)
                    normalise(0)
                    p_lo(1)
                    stats_c(0, 0, 0)
                    normalise(1)
                    dq_masks(4, 8)
                    p_lo(2)
                    norm_c(0, 0, first=True)
                    normalise(2)
                    p_lo(3)
                    normalise(3)
                    lo8(xc_t[:, 0], M[2], M[3], S["cxt_hi"], S["cxt_lo"], 0, XS)
                    lo8(o_t, M[0], M[1], S["ot_hi"], S["ot_lo"], 2 * t, 1.0)
                    dve.wait_ge(S["lut_loaded"], 16 * t + 16)
                    dq_rest(8, 12)
                    dq_rest(12, 16)
                    dve.wait_ge(S["bias_loaded"], 16)
                    bias_c(0, 0)
                    dve.wait_ge(S["res_loaded"], 16 * t + 16)
                    residual(0)
                    residual(1)
                    dq_lo()
                    return

                if att:
                    masked(0)
                    dq_index()
                    masked(1)
                if qkv:
                    rotate_half(u, 0, G[0], S["q_scaled"], S["q_rotated"])
                if att:
                    dq_nibbles()
                    dq_masks(0, 4)
                    p_lo(0)
                    masked(2)
                if qkv:
                    rotate_half(u, 1, G[1], S["q_scaled"], S["q_rotated"])
                if att:
                    normalise(0)
                    masked(3)
                    p_lo(1)
                if ln:
                    norm_stats_b(t + 2)
                if att:
                    dq_masks(4, 8)
                if qkv:
                    lo8(q_t, M[0], M[1], S["qt_hi"], S["qt_lo"], 2 * u, 1.0)
                    if not att:
                        pieces_lo(3 * KT, 3 * KT + KT // 2)
                    rotate_half(u, 0, G[2], S["k_scaled"], S["k_rotated"])
                if att:
                    normalise(1)
                    p_lo(2)
                if ln:
                    norm_b(t + 2)
                if att:
                    dq_masks(8, 12)
                if qkv:
                    rotate_half(u, 1, G[0], S["k_scaled"], S["k_rotated"])
                if att:
                    normalise(2)
                    p_lo(3)
                    normalise(3)
                    dq_masks(12, 16)
                if qkv:
                    lo8(k_t, M[2], M[3], S["kt_hi"], S["kt_lo"], 2 * u, 1.0)
                    values_half(u, 0, G[1])
                if att:
                    lo8(o_t, M[0], M[1], S["ot_hi"], S["ot_lo"], 2 * t, 1.0)
                if qkv:
                    values_half(u, 1, G[2])
                if ln:
                    lo8(x_t, M[2], M[3], S["xt_hi"], S["xt_lo"], 2 * t + 4, XS)
                if att:
                    dve.wait_ge(S["res_loaded"], 16 * t + 16)
                    residual(0)
                    dq_lo()
                    residual(1)

            dve.wait_ge(S["const_loaded"], 64)
            norm_stats_b(0)
            norm_b(0)
            lo8(x_t, M[2], M[3], S["xt_hi"], S["xt_lo"], 0, XS)
            pieces_lo(2 * KT, 3 * KT)
            norm_stats_b(1)
            norm_b(1)
            body(-1, False, True, False)
            lo8(x_t, M[2], M[3], S["xt_hi"], S["xt_lo"], 2, XS)
            pieces_lo(3 * KT + KT // 2, PIECES)
            dve.wait_ge(S["w_lo"], PIECES)
            body(0, True, True, True)
            with dve.Fori(1, TILES - 2) as t:
                body(t, True, True, True)
            body(TILES - 2, True, True, False)
            body(TILES - 1, True, False, False)

            def sum_half(t, slot, half):
                if half == 0:
                    dve.wait_ge(S["cb_ready"], t + 1)
                dve.wait_ge(S["f_pe"], 2 * t + half + 1)
                r = hc[:, slot, half * HALF:(half + 1) * HALF]
                bank = ((G[2], M[2]), (G[0], G[1]))[slot % 2][half]
                V.scalar_tensor_tensor(r, bank[:, :], 1.0 / (XS * WS), r, ALU.mult, ALU.add).then_inc(S["f_out"], 1)

            stats_c(1, 0, 1)
            norm_c(1, 1, first=True)
            bias_c(1, 1)

            def four(g, last=False):
                for slot in range(SLOTS):
                    t = SLOTS * g + slot
                    sum_half(t, slot, 0)
                    if not last or slot < SLOTS - 1:
                        lo8(xc_t[:, 1 - slot % 2], M[0], M[1], S["cxt_hi"], S["cxt_lo"], 2 * t + 2, XS)
                    if not last or slot < SLOTS - 2:
                        stats_c(t + 2, g + (slot + 2) // SLOTS, (slot + 2) % SLOTS)
                        norm_c(t + 2, (slot + 2) % SLOTS)
                        bias_c(t + 2, (slot + 2) % SLOTS)
                    sum_half(t, slot, 1)
            with dve.Fori(0, TILES // SLOTS - 1) as g:
                four(g)
            four(TILES // SLOTS - 1, last=True)

        @block.gpsimd
        def _(pool):
            Gp = nc.gpsimd

            full = [P, T, JM]
            pool.wait_ge(S["ab_loaded"], 48)
            Gp.tensor_tensor(powers, abslog.unsqueeze(2).broadcast_to(full), mults_s.unsqueeze(1).broadcast_to(full),
                             ALU.mult).then_inc(S["logs_ready"], 1)
            shape = [P, T, 2, L3]
            x12 = table[:, :, 0:2 * L3].rearrange("p t (two n) -> p t two n", two=2)
            pool.wait_ge(S["powers_ready"], 1)
            pool.wait_ge(S["table_sin"], 9)
            Gp.tensor_tensor(x12, x12, powers[:, :, XC].unsqueeze(2).broadcast_to(shape), ALU.mult).then_inc(S["x_ready"], 1)
            pool.wait_ge(S["gp_ready"], 1)
            pool.wait_ge(S["table_ready"], 3)
            pool.wait_ge(S["x_ready"], 1)

            def four_chunks(g, first=False):
                for k in range(STAGES):
                    n, par = STAGES * g + k, k % 2
                    hs = bass.ds(n * HC, HC)
                    sq, sw = [P, HC, L3, L4], [P, HC, L1, IMAGES]
                    pool.wait_ge(S[f"c_loaded_{k}"], 16 * (g + 1))
                    if not (first and k < 2):
                        pool.wait_ge(S["w_ready"], n - 1)
                    Gp.tensor_tensor(w_tmp[:, par].rearrange("p h (a b) -> p h a b", b=IMAGES),
                                     c_in[:, k, :, 1].unsqueeze(2).broadcast_to(sw),
                                     gp2[:, hs].unsqueeze(3).broadcast_to(sw), ALU.mult).then_inc(S["wt_mult"], 1)
                    if not (first and k < 2):
                        pool.wait_ge(S["mixed"], 2 * (n - 1))
                    Gp.tensor_tensor(q2_pow[:, par].rearrange("p h (a b) -> p h a b", b=L4),
                                     table[:, hs, col("x2")].unsqueeze(3).broadcast_to(sq),
                                     table[:, hs, col("y2")].unsqueeze(2).broadcast_to(sq), ALU.mult).then_inc(S["q2_ready"], 1)
            four_chunks(0, True)
            with pool.Fori(1, CHUNKS // STAGES) as g:
                four_chunks(g)

            def inv_std(t, var, mean_var, r, done, step):
                pool.wait_ge(var, t + 1)
                Gp.tensor_tensor(r[:, 0:1], mean_var[:, 1:2], eps[:], ALU.add).then_inc(step, 1)
                pool.wait_ge(step, t + 1)
                Gp.tensor_tensor(r[:, 1:2], r[:, 0:1], minus_half[:], ALU.pow).then_inc(done, 1)


            def body(t, att, ln):
                def dq_adds(v0, v1):
                    for v in range(v0, v1):
                        pool.wait_ge(S["dq_termed"], LUT * t + v + 1)
                        if v > 1:
                            pool.wait_ge(S["dq_sum"], TERMS * t + v - 1)
                        Gp.tensor_tensor(dq_w, dq_w, dq_term[:, v % 2], ALU.add).then_inc(S["dq_sum"], 1)

                def less_max(c):
                    pool.wait_ge(S["s_max"], 4 * t + c + 1)
                    Gp.tensor_tensor(scores[:, c % 2], scores[:, c % 2], mx[:, c % 2].unsqueeze(2).broadcast_to([P, CH, T]),
                                     ALU.subtract).then_inc(S["s_sub"], 1)

                if att:
                    less_max(0)
                    less_max(1)
                    dq_adds(1, 2)
                    less_max(2)
                    dq_adds(2, 4)
                    less_max(3)
                if ln:
                    inv_std(t + 2, S["var_ready"], mv, rstd, S["rstd_ready"], S["var_eps_ready"])
                elif isinstance(t, int) and t == TILES - 1:
                    inv_std(0, S["cvar_ready"], mvc, rstdc, S["crstd_ready"], S["cvar_eps_ready"])
                if att:
                    dq_adds(4, LUT // 2 if isinstance(t, int) and t == TILES - 1 else LUT)
            inv_std(0, S["var_ready"], mv, rstd, S["rstd_ready"], S["var_eps_ready"])
            for par in range(2):
                pool.wait_ge(S[f"h0_stored_{par}"], 16 * CHUNKS // 2)
            pool.wait_ge(S["w_ready"], CHUNKS)
            Gp.memset(v_hi[:, :, HD:VW], 1.0)
            Gp.memset(v_lo[:, :, HD:VW], 0.0)
            Gp.memset(probs, 0.0).then_inc(S["zeros_ready"], 1)
            inv_std(1, S["var_ready"], mv, rstd, S["rstd_ready"], S["var_eps_ready"])
            body(0, True, True)
            with pool.Fori(1, TILES - 2) as t:
                body(t, True, True)
            body(TILES - 2, True, False)
            body(TILES - 1, True, False)

            with pool.Fori(1, TILES) as t:
                inv_std(t, S["cvar_ready"], mvc, rstdc, S["crstd_ready"], S["cvar_eps_ready"])


def kernel(x, L0_tok_A_abslog, L0_tok_A_phase, L0_attn_wq, L0_attn_wk, L0_attn_wv, L0_attn_wo, L0_ffn_qweight,
           L0_ffn_lut4, L0_ffn_lut8, L0_ffn_bias):
    import concourse.bacc as bacc
    from concourse.bass_utils import run_bass_kernel_spmd

    def lay(v):
        return np.ascontiguousarray(v)

    arrays = {
        "c_t": lay(np.tile(np.asarray(x).transpose(2, 1, 3, 0).reshape(N, CHUNKS, HC, 2, IMAGES).transpose(1, 0, 2, 3, 4),
                           (1, 2, 1, 1, 1))),
        "abslog_t": lay(np.tile(np.asarray(L0_tok_A_abslog).T, (2, 1))),
        "phase_t": lay(np.tile(np.asarray(L0_tok_A_phase).T, (2, 1))),
        "w_t": lay(np.stack([np.asarray(w).T.reshape(KT, P, L) for w in (L0_attn_wq, L0_attn_wk, L0_attn_wv, L0_attn_wo)])
                   .reshape(PIECES, P, L)),
        "qwords": lay(np.asarray(L0_ffn_qweight)[0:PLANES].reshape(PLANES, L // P, P, 2, WORDS).transpose(1, 3, 2, 0, 4)
                      .reshape(DQ_STEPS, P, PLANES, WORDS)),
        "lut4_steps": lay(np.repeat(np.asarray(L0_ffn_lut4).reshape(L // P, P, LUT), 2, axis=0)),
        "bias_rows": lay(np.broadcast_to(np.asarray(L0_ffn_bias)[None, :], (P, L))),
        **shape_constants(),
    }
    nc = bacc.Bacc("TRN2", target_bir_lowering=False, num_devices=1)
    aps = {n: nc.dram_tensor("in_" + n, v.shape, mybir.dt.from_np(v.dtype), kind="ExternalInput").ap() for n, v in arrays.items()}
    out = nc.dram_tensor("out_h", (TILES, P, L), F32, kind="ExternalOutput").ap()
    build(nc, aps, out)
    r = run_bass_kernel_spmd(nc, [{"in_" + n: v for n, v in arrays.items()}], core_ids=[0])
    return r.results[0]["out_h"].reshape(IMAGES, T, L)
```
